# Optimizing a Trainium2 kernel written in Bass

```python
import numpy as np
import jax
import jax.numpy as jnp

def _softmax(x, axis=-1):
    return jax.nn.softmax(x, axis=axis)

def _gelu(x):
    return jax.nn.gelu(x, approximate=True)

def _silu(x):
    return jax.nn.silu(x)

def _sigmoid(x):
    return jax.nn.sigmoid(x)

def _layernorm(x, axis=-1, eps=1e-05):
    m = jnp.mean(x, axis=axis, keepdims=True)
    v = jnp.var(x, axis=axis, keepdims=True)
    return (x - m) / jnp.sqrt(v + eps)

def _scatter_add(tgt, idx, src, axis=0):
    return tgt.at[idx].add(src)

def _segment_sum(src, seg, n):
    return jax.ops.segment_sum(src, seg, n)
kernel_name = 'mk_adaln_d1_jaxref_r8_71baa8'

def setup_inputs(seed: int=0):
    np.random.seed(seed)
    _w = jnp.asarray

    def _L0_attn_setup():
        import jax, jax.numpy as jnp
        import numpy as np
        HIDDEN = 256
        KEY = 256
        EPS = 1e-05
        key = jax.random.key(seed)
        k1, k2, k3 = jax.random.split(key, 3)
        B, S = (4, 256)
        x = jax.random.normal(k1, (B, S, HIDDEN), dtype=jnp.float32)
        bq = 1.0 / np.sqrt(HIDDEN)
        qkv = jax.random.uniform(k2, (HIDDEN, KEY * 3), minval=-bq, maxval=bq, dtype=jnp.float32)
        bo = 1.0 / np.sqrt(KEY)
        o_proj = jax.random.uniform(k3, (KEY, HIDDEN), minval=-bo, maxval=bo, dtype=jnp.float32)
        gamma = jnp.ones((HIDDEN,), dtype=jnp.float32)
        beta = jnp.zeros((HIDDEN,), dtype=jnp.float32)
        return {'x': x, 'qkv': qkv, 'o_proj': o_proj, 'gamma': gamma, 'beta': beta}
    _L0_attn_in = _L0_attn_setup()

    def _L0_ffn_setup():
        import jax, jax.numpy as jnp
        import numpy as np
        TOP_K = 4
        key = jax.random.key(seed)
        ks = jax.random.split(key, 8)
        B, S, D, E, H, HS = (2, 256, 256, 16, 128, 512)
        scaled = lambda k, shape, fan: jax.random.normal(k, shape, jnp.float32) * fan ** (-0.5)
        return {'x': jax.random.normal(ks[0], (B, S, D), jnp.float32), 'w_router': scaled(ks[1], (D, E), D), 'we1': scaled(ks[2], (E, D, H), D), 'we3': scaled(ks[3], (E, D, H), D), 'we2': scaled(ks[4], (E, H, D), H), 'ws1': scaled(ks[5], (D, HS), D), 'ws3': scaled(ks[6], (D, HS), D), 'ws2': scaled(ks[7], (HS, D), HS)}
    _L0_ffn_in = _L0_ffn_setup()
    _L0_c = _w((lambda *s: np.random.randn(*s).astype(np.float32) * 0.05)(2, 256))
    _L0_wmod = _w((lambda *s: np.random.randn(*s).astype(np.float32) * 0.05)(256, 6 * 256) * 256 ** (-0.5))
    _d = {'L0_attn_x': _L0_attn_in['x'], 'L0_attn_qkv': _L0_attn_in['qkv'], 'L0_attn_o_proj': _L0_attn_in['o_proj'], 'L0_attn_gamma': _L0_attn_in['gamma'], 'L0_attn_beta': _L0_attn_in['beta'], 'L0_ffn_w_router': _L0_ffn_in['w_router'], 'L0_ffn_we1': _L0_ffn_in['we1'], 'L0_ffn_we3': _L0_ffn_in['we3'], 'L0_ffn_we2': _L0_ffn_in['we2'], 'L0_ffn_ws1': _L0_ffn_in['ws1'], 'L0_ffn_ws3': _L0_ffn_in['ws3'], 'L0_ffn_ws2': _L0_ffn_in['ws2'], 'L0_c': _L0_c, 'L0_wmod': _L0_wmod}
    _x0 = _d['L0_attn_x']
    _d['L0_attn_x'] = jax.random.normal(jax.random.fold_in(jax.random.key(seed), 1), (2, 1024, 256), dtype=_x0.dtype)
    del _x0
    return _d

def reference(L0_attn_x, L0_attn_qkv, L0_attn_o_proj, L0_attn_gamma, L0_attn_beta, L0_ffn_w_router, L0_ffn_we1, L0_ffn_we3, L0_ffn_we2, L0_ffn_ws1, L0_ffn_ws3, L0_ffn_ws2, L0_c, L0_wmod):

    def _L0_attn_ref(x, qkv, o_proj, gamma, beta):
        import jax, jax.numpy as jnp
        import numpy as np
        HIDDEN = 256
        KEY = 256
        EPS = 1e-05
        residual = x
        mu = jnp.mean(x, axis=-1, keepdims=True)
        var = jnp.mean((x - mu) ** 2, axis=-1, keepdims=True)
        x_norm = (x - mu) / jnp.sqrt(var + EPS) * gamma + beta
        q = x_norm @ qkv[:, :KEY]
        k = x_norm @ qkv[:, KEY:2 * KEY]
        v = x_norm @ qkv[:, 2 * KEY:]
        scale = 1.0 / jnp.sqrt(jnp.float32(KEY))
        scores = jnp.einsum('bsk,btk->bst', q, k) * scale
        S_len = x.shape[1]
        causal = jnp.tril(jnp.ones((S_len, S_len), dtype=bool))
        scores = jnp.where(causal[None], scores, -jnp.inf)
        attn = jax.nn.softmax(scores, axis=-1)
        out = attn @ v
        out = out @ o_proj
        return out + residual

    def _L0_ffn_ref(x, w_router, we1, we3, we2, ws1, ws3, ws2):
        import jax, jax.numpy as jnp
        import numpy as np
        TOP_K = 4
        B, S, D = x.shape
        T = B * S
        E = w_router.shape[1]
        xt = x.reshape(T, D)
        probs = jax.nn.softmax(xt @ w_router, axis=-1)
        top_w, top_i = jax.lax.top_k(probs, TOP_K)
        top_w = top_w / jnp.sum(top_w, axis=-1, keepdims=True)
        cw = jnp.zeros((T, E), xt.dtype).at[jnp.arange(T)[:, None], top_i].add(top_w)
        g = jax.nn.silu(jnp.einsum('td,edh->teh', xt, we1)) * jnp.einsum('td,edh->teh', xt, we3)
        g = g * cw[:, :, None]
        moe_out = jnp.einsum('teh,ehd->td', g, we2)
        shared = jax.nn.silu(xt @ ws1) * (xt @ ws3) @ ws2
        k = TOP_K
        out = shared / (k + 1) + moe_out * (k / (k + 1))
        return out.reshape(B, S, D)
    x = L0_attn_x
    mod = (_silu(L0_c) @ L0_wmod).reshape(L0_c.shape[0], 6, 1, -1)
    sa, ca, ga, sb, cb, gb = (mod[:, 0], mod[:, 1], mod[:, 2], mod[:, 3], mod[:, 4], mod[:, 5])
    ga = (2 * (ga >= 0) - 1) * jnp.maximum(jnp.abs(ga), 0.25)
    gb = (2 * (gb >= 0) - 1) * jnp.maximum(jnp.abs(gb), 0.25)
    h = _layernorm(x, axis=-1) * (1 + ca) + sa
    x = x + ga * _L0_attn_ref(h, L0_attn_qkv, L0_attn_o_proj, L0_attn_gamma, L0_attn_beta)
    h = _layernorm(x, axis=-1) * (1 + cb) + sb
    x = x + gb * _L0_ffn_ref(h, L0_ffn_w_router, L0_ffn_we1, L0_ffn_we3, L0_ffn_we2, L0_ffn_ws1, L0_ffn_ws3, L0_ffn_ws2)
    return x

_drawn_inputs = setup_inputs


def setup_inputs(seed=0):
    import zlib

    import numpy as np

    out = dict(_drawn_inputs(seed))
    spreads = {'L0_attn_gamma': (1.0, 0.6), 'L0_attn_beta': (0.0, 0.8)}
    factors = {'L0_attn_qkv': 5.127,
     'L0_attn_o_proj': 5.288,
     'L0_ffn_w_router': 3.585,
     'L0_ffn_we1': 3.366,
     'L0_ffn_we3': 3.273,
     'L0_ffn_we2': 3.227,
     'L0_ffn_ws1': 7.321,
     'L0_ffn_ws3': 6.899,
     'L0_ffn_ws2': 6.845}
    for name, (base, spread) in spreads.items():
        noise = np.random.default_rng([zlib.crc32(name.encode()), seed]).standard_normal(out[name].shape)
        drawn = base * np.exp(spread * noise) if base else spread * noise
        out[name] = jnp.asarray(drawn.astype(out[name].dtype))
    for name, factor in factors.items():
        out[name] = (out[name] * factor).astype(out[name].dtype)
    return out
```

```python
from contextlib import ExitStack

import concourse.bass as bass
from concourse import mybir

F32 = mybir.dt.float32
F32R = mybir.dt.float32r
ALU = mybir.AluOpType
ACT = mybir.ActivationFunctionType
AX = mybir.AxisListType

P = 128
D = 256
DC = D // P
B, S = 2, 1024
T = B * S
NT = S // P
E = 16
TOPK = 4
H = 128
HS = 512
SH = HS // H
EX = SH + E
TB = 512
NB = T // TB
BT = TB // P
EPS = 1e-5
BANK = 512
MASKED = -1e30
GATE_FLOOR = 0.25

W1, W3, W2, WX = 0, D, 2 * D, 3 * D
UN = 4
NG = EX // UN
CREDIT = 4

HEADROOM = 4


def units_of(i):
    first = i if i < BT else BT + 2 * (i - BT)
    return [(first + n // BT, n, min(BT, i + 1 - n)) for n in range(0, i + 1, BT)]


UNITS = units_of(NT - 1)[-1][0] + 1
PT_RING = 3
R_SHIFTED = T // P + 1
R_DONE = R_SHIFTED + 15


def at(b, i):
    return b * NT + (i + 1 + CREDIT)


def at_row(b):
    return b + (1 + CREDIT)


def before_row(b):
    return b + CREDIT


def at_unit(b, u):
    return b * UNITS + (u + 1 + CREDIT)


def adaln_block(nc, x, qkv, o_proj, gamma, beta, w_router, we1, we3, we2, ws1, ws3, ws2, c_in, wmod, out):
    cw_dram = nc.dram_tensor("cw_rows", (EX, T), F32, kind="Internal").ap()
    ctx = ExitStack()
    with ctx:
        def sb(name, shape, dt=F32):
            return ctx.enter_context(nc.sbuf_tensor(name, shape, dt))

        def sem(name):
            return ctx.enter_context(nc.semaphore(name))

        w_raw = sb("w_raw", [P, EX, WX])
        h2T_hi = sb("h2T_hi", [P, DC, T], F32R)
        h2T_lo = sb("h2T_lo", [P, DC, T], F32R)
        x1 = sb("x1", [P, B * NT, D])
        mod = sb("mod", [P, B, 5 * D])
        gate_b = sb("gate_b", [P, NB, D])
        ident = sb("ident", [P, P])
        ident_r = sb("ident_r", [P, P], F32R)
        mask_r = sb("mask_r", [P, P], F32R)
        wr_hi = sb("wr_hi", [P, DC, P], F32R)
        wr_lo = sb("wr_lo", [P, DC, P], F32R)
        logits = sb("logits", [P, B * NT, E])
        cols = sb("cols", [P, 4, DC])
        silu_c = sb("silu_c", [P, B, DC])
        minus_half = sb("minus_half", [P, 1])
        eps = sb("eps", [P, 1])
        bn = sb("bn", [P, 3, 4, 6])
        mv = sb("mv", [P, 3, 4, 2])
        veps = sb("veps", [P, 3, 4])
        rstd = sb("rstd", [P, 3, 4])
        negmax = sb("negmax", [P, 4])
        rowsum = sb("rowsum", [P, 4])
        rinv = sb("rinv", [P, 4])

        rpool = sb("rpool", [P, 15360], F32R)

        def r_part(at_, n):
            return rpool[:, at_:at_ + n]

        xnT_hi = r_part(0, 2048).rearrange("p (c t) -> p c t", c=DC)
        xnT_lo = r_part(2048, 2048).rearrange("p (c t) -> p c t", c=DC)
        v_hi = r_part(4096, 2048).rearrange("p (t d) -> p t d", d=D)
        v_lo = r_part(6144, 2048).rearrange("p (t d) -> p t d", d=D)
        pT_hi = r_part(8192, 1536).rearrange("p (u k) -> p u k", k=BANK)
        pT_lo = r_part(9728, 1536).rearrange("p (u k) -> p u k", k=BANK)
        qT_hi = r_part(11264, 512).rearrange("p (s c t) -> p s c t", s=2, c=DC)
        qT_lo = r_part(11776, 512).rearrange("p (s c t) -> p s c t", s=2, c=DC)
        wqk_hi = r_part(12288, 512).rearrange("p (c d) -> p c d", c=DC)
        wqk_lo = r_part(12800, 512).rearrange("p (c d) -> p c d", c=DC)
        wvo_hi = r_part(13312, 1024).rearrange("p (b c d) -> p b c d", b=B, c=DC)
        wvo_lo = r_part(14336, 1024).rearrange("p (b c d) -> p b c d", b=B, c=DC)
        w_hi = r_part(0, UN * WX).rearrange("p (s w) -> p s w", s=UN)
        w_lo = r_part(3072, UN * WX).rearrange("p (s w) -> p s w", s=UN)
        g_hi = r_part(6144, 2 * TB).rearrange("p (s t) -> p s t", s=2)
        g_lo = r_part(7168, 2 * TB).rearrange("p (s t) -> p s t", s=2)

        fpool = sb("fpool", [P, 5120])

        def f_part(at_, n):
            return fpool[:, at_:at_ + n]

        probs = f_part(0, 2048).rearrange("p (s k) -> p s k", s=2)
        x_in = f_part(2048, 1024).rearrange("p (s d) -> p s d", s=4)
        zx = f_part(3072, 512).rearrange("p (s d) -> p s d", s=2)
        h = f_part(3584, 512).rearrange("p (s d) -> p s d", s=2)
        xf = f_part(4096, 512).rearrange("p (s c t) -> p s c t", s=2, c=DC)
        h2 = f_part(4608, 512).rearrange("p (s d) -> p s d", s=2)
        shared_w = fpool[0:SH, 0:T]
        gate_tmp = f_part(4096, 256)
        wr_raw = f_part(3584, DC * P).rearrange("p (c e) -> p c e", c=DC)
        logitsT = f_part(0, S)
        silu_b = f_part(4608, 512).rearrange("p (b c q) -> p b c q", b=B, c=DC)
        act_g = f_part(0, 2 * TB).rearrange("p (s t) -> p s t", s=2)
        cwb = f_part(1024, 4 * TB).rearrange("p (s t) -> p s t", s=4)
        yT = f_part(3072, DC * TB).rearrange("p (c t) -> p c t", c=DC)
        y_out = f_part(4096, BT * D).rearrange("p (t d) -> p t d", t=BT)
        cwT = fpool[0:E, 3072:3072 + T]
        LATE = 11
        stage = w_raw[:, LATE:EX, :].rearrange("p e w -> p (e w)")
        wmod_sb = stage[:, 0:DC * 6 * D].rearrange("p (c n) -> p c n", c=DC)
        qkv_sb = stage[:, 3072:3072 + DC * 3 * D].rearrange("p (c n) -> p c n", c=DC)
        o_sb = stage[:, 4608:4608 + DC * D].rearrange("p (c n) -> p c n", c=DC)
        wT_sb = stage[:, 5120:5120 + 3 * DC * D].rearrange("p (m k c) -> p m k c", m=3, k=DC)
        rt = mod[:, :, :].rearrange("p b n -> p (b n)")
        top8 = rt[:, 0:128].rearrange("p (t k) -> p t k", k=8)
        above = rt[:, 128:384].rearrange("p (t e) -> p t e", e=E)
        ties = rt[:, 384:640].rearrange("p (t e) -> p t e", e=E)
        nth_tie = rt[:, 640:896].rearrange("p (t e) -> p t e", e=E)
        expd = rt[:, 896:1152].rearrange("p (t e) -> p t e", e=E)
        reset = rt[:, 1152:1408].rearrange("p (t e) -> p t e", e=E)
        cw = rt[:, 1408:1664].rearrange("p (t e) -> p t e", e=E)
        need = rt[:, 1664:1680].rearrange("p (t e) -> p t e", e=1)
        total = rt[:, 1680:1696].rearrange("p (t e) -> p t e", e=1)

        ps = ctx.enter_context(nc.psum_tensor("ps", [P, 8, BANK], F32))
        Y0, Y1, X0, TR = 6, 7, 4, 6

        def score_banks(i):
            return ps[:, 2 * (i % 2):2 * (i % 2) + 2, :].rearrange("p b n -> p (b n)")[:, 0:(i + 1) * P]

        s_ld_c, s_ld_cols, s_ld_qkv, s_ld_o, s_ld_wr = (sem(n) for n in (
            "ld_c", "ld_cols", "ld_qkv", "ld_o", "ld_wr"))
        s_ld_wmod = [sem(f"ld_wmod{n}") for n in range(3)]
        s_ld_w = sem("ld_w_early")
        s_ld_w2 = sem("ld_w_late")
        s_x = [sem(f"x_loaded{n}") for n in range(4)]
        s_cwb = [sem(f"weights_bcast{n}") for n in range(4)]
        s_shared = sem("shared_rows_stored")
        s_cwst = sem("cw_rows_stored")
        s_out = sem("out_stored")
        s_const, s_siluc, s_silub, s_mod_mm, s_modev, s_gt, s_wt_mm, s_wt_a, s_wt_d = (sem(n) for n in (
            "const", "siluc", "silub", "mod_mm", "mod_evac", "gate_chain", "wT_mm", "wT_act", "wT_dve"))
        s_wr0 = sem("router_pad_zeroed")
        s_constr, s_wqk_mm, s_wvo_mm, s_wsp_a, s_wsp_d, s_wvf = (sem(n) for n in (
            "const_r", "wqk_mm", "wvo_mm", "wsplit_hi", "wsplit_lo", "wvo_gated"))
        dve_tile = {n: sem("t_" + n) for n in (
            "bn1", "stat1", "z", "bn2", "stat2", "xn", "xlo", "negmax", "qlo", "vlo", "ptlo", "rinv", "x1",
            "bn3", "stat3", "z2", "hlo")}
        pool_tile = {n: sem("t_" + n) for n in (
            "eps1", "rstd1", "hmul", "h", "eps2", "rstd2", "rmul", "resid", "eps3", "rstd3", "h2mul", "h2")}
        pe_tile = {n: sem("t_" + n) for n in ("xT", "qv", "scores", "pT", "h2T", "pv")}
        act_tile = {n: sem("t_" + n) for n in ("xf", "xhi", "exp", "qhi", "vhi", "pthi", "hhi")}
        s_lgT_mm, s_lgT, s_lg_mm, s_lg = (sem(n) for n in ("logitsT_mm", "logitsT", "logits_mm", "logits_evac"))
        tl = {**dve_tile, **pool_tile, **pe_tile, **act_tile}
        s_rt, s_rexp, s_cwT_mm, s_cwT_a, s_cwT_d = (sem(n) for n in (
            "router_chain", "router_exp", "cwT_mm", "cwT_act", "cwT_dve"))
        s_whi, s_wlo, s_ab, s_y, s_silu, s_up, s_g, s_ghi, s_glo = (sem(n) for n in (
            "w_hi", "w_lo", "gate_up_mm", "down_mm", "silu", "up_mul", "g", "g_hi", "g_lo"))
        s_ya, s_yd, s_yT_mm, s_gated, s_final = (sem(n) for n in (
            "y_evac_act", "y_evac_dve", "y_back", "y_gated", "y_final"))

        x_t = x.rearrange("b (i p) d -> b i p d", p=P)
        out_t = out.rearrange("b (n t p) d -> (b n) p t d", t=BT, p=P)

        block = ctx.enter_context(nc.Block())

        @block.sync
        def _(sp):
            with nc.allow_non_contiguous_dma(reason="small column loads"):
                for b in range(B):
                    sp.dma_start(cols[:, 2 + b, :], c_in[b].rearrange("(c p) -> p c", p=P)).then_inc(s_ld_c, 16)
                sp.dma_start(cols[:, 0, :], gamma.rearrange("(c p) -> p c", p=P)).then_inc(s_ld_cols, 16)
                sp.dma_start(cols[:, 1, :], beta.rearrange("(c p) -> p c", p=P)).then_inc(s_ld_cols, 16)
            sp.dma_start(wmod_sb[:, :, 2 * D:4 * D], wmod[:, 2 * D:4 * D].rearrange("(c p) n -> p c n", p=P)
                         ).then_inc(s_ld_wmod[1], 16)
            with sp.Fori(0, B) as b:
                for i in range(NT):
                    sp.wait_ge(tl["resid"], at(b, i - 4))
                    sp.dma_start(x_in[:, i % 4, :], x_t[bass.ds(b, 1), i].rearrange("a p d -> (a p) d")
                                 ).then_inc(s_x[i % 4], 16)
            sp.wait_ge(s_cwT_a, 1)
            sp.wait_ge(s_cwT_d, 1)
            sp.dma_start(cw_dram[SH:EX, :], cwT).then_inc(s_cwst, 16)
            sp.wait_ge(s_shared, 16)
            sp.wait_ge(tl["resid"], at(B - 1, NT - 1))
            sp.wait_ge(tl["xT"], at(B - 1, NT - 1))

            def weights(b, e, k, n):
                if not (isinstance(n, int) and n < 4):
                    sp.wait_ge(s_g, n - 4 + 1)
                row = cw_dram[e:e + 1, :] if isinstance(e, int) else cw_dram[bass.ds(e, 1), :]
                cut = row[:, b * TB:(b + 1) * TB] if isinstance(b, int) else row[:, bass.ds(b * TB, TB)]
                sp.dma_start(cwb[:, k, :], cut.broadcast_to((P, TB))).then_inc(s_cwb[k], 16)

            def store(b):
                sp.wait_ge(s_final, b + 1)
                dst = out_t[b] if isinstance(b, int) else out_t[bass.ds(b, 1)].rearrange("a p t d -> (a p) t d")
                sp.dma_start(dst, y_out).then_inc(s_out, 16)

            def group(b, g):
                for k in range(UN):
                    e = g * UN + k
                    weights(b, e, k, b * EX + e)

            def rest(b):
                with sp.Fori(1, NG - 1) as g:
                    group(b, g)
                group(b, NG - 1)

            group(0, 0)
            sp.wait_ge(s_cwst, 16)
            rest(0)
            with sp.Fori(1, NB) as b:
                group(b, 0)
                rest(b)
                store(b - 1)
            store(NB - 1)
            sp.wait_ge(s_out, 16 * NB)

        @block.gpsimd
        def _(pool):
            for s in pool_tile.values():
                pool.sem_inc(s, CREDIT)
            nc.gpsimd.memset(ident[:], 1.0).then_inc(s_const, 1)
            nc.gpsimd.memset(x1[:, 0, 0:P], 0.0).then_inc(s_const, 1)
            nc.gpsimd.memset(eps[:], EPS).then_inc(s_const, 1)
            nc.gpsimd.memset(minus_half[:], -0.5).then_inc(s_const, 1)
            nc.gpsimd.memset(shared_w, 1.0 / (TOPK + 1)).then_inc(s_const, 1)
            nc.gpsimd.memset(wr_raw, 0.0).then_inc(s_wr0, 1)
            pool.wait_ge(s_const, 5)
            nc.gpsimd.affine_select(out=ident[:], in_=ident[:], compare_op=ALU.is_equal, fill=0.0, base=0,
                                    pattern=[[-1, P]], channel_multiplier=1).then_inc(s_const, 1)
            nc.gpsimd.affine_select(out=x1[:, 0, 0:P], in_=x1[:, 0, 0:P], compare_op=ALU.is_ge, fill=MASKED,
                                    base=0, pattern=[[-1, P]], channel_multiplier=1).then_inc(s_const, 1)

            def inverse_std(which, b, i, mean_var, need_before):
                pool.wait_ge(tl[mean_var], at(b, i))
                pool.wait_ge(tl[need_before], at(b, i - 4))
                n = which + 1
                nc.gpsimd.tensor_tensor(veps[:, which, i % 4:i % 4 + 1], mv[:, which, i % 4, 1:2], eps[:],
                                        ALU.add).then_inc(tl[f"eps{n}"], 1)
                pool.wait_ge(tl[f"eps{n}"], at(b, i))
                nc.gpsimd.tensor_tensor(rstd[:, which, i % 4:i % 4 + 1], veps[:, which, i % 4:i % 4 + 1],
                                        minus_half[:], ALU.pow).then_inc(tl[f"rstd{n}"], 1)

            def mod_row(b, n):
                return mod[:, bass.ds(b, 1), n * D:(n + 1) * D].rearrange("p a d -> p (a d)")

            pool.wait_ge(s_constr, 2)
            with pool.Fori(0, B) as b:
                for s in range(-HEADROOM, NT + 2):
                    t = s + 4
                    if t < NT:
                        inverse_std(0, b, t, "stat1", "z")
                    t = s - 2
                    if 0 <= t < NT:
                        pool.wait_ge(tl["z2"], at(b, t))
                        pool.nop(nofuse=True)
                        nc.gpsimd.tensor_tensor(h2[:, t % 2, :], h2[:, t % 2, :], mod_row(b, 4), ALU.mult
                                                ).then_inc(tl["h2mul"], 1)
                        pool.wait_ge(tl["h2mul"], at(b, t))
                        pool.nop(nofuse=True)
                        nc.gpsimd.tensor_tensor(h2[:, t % 2, :], h2[:, t % 2, :], mod_row(b, 3), ALU.add
                                                ).then_inc(tl["h2"], 1)
                    t = s + 4
                    if t < NT:
                        pool.wait_ge(tl["z"], at(b, t))
                        pool.wait_ge(s_modev, 1)
                        pool.wait_ge(tl["xn"], at(b, t - 2))
                        pool.nop(nofuse=True)
                        nc.gpsimd.tensor_tensor(h[:, t % 2, :], zx[:, t % 2, :], mod_row(b, 1), ALU.mult
                                                ).then_inc(tl["hmul"], 1)
                        pool.wait_ge(tl["hmul"], at(b, t))
                        pool.nop(nofuse=True)
                        nc.gpsimd.tensor_tensor(h[:, t % 2, :], h[:, t % 2, :], mod_row(b, 0), ALU.add
                                                ).then_inc(tl["h"], 1)
                    t = s + 3
                    if 0 <= t < NT:
                        inverse_std(1, b, t, "stat2", "xn")
                        x1_t = x1[:, bass.ds(b * NT + t, 1), :].rearrange("p a d -> p (a d)")
                        pool.wait_ge(tl["h"], at(b, t))
                        pool.wait_ge(s_modev, 3)
                        pool.nop(nofuse=True)
                        nc.gpsimd.tensor_tensor(x1_t, h[:, t % 2, :], mod_row(b, 2), ALU.mult
                                                ).then_inc(tl["rmul"], 1)
                        pool.wait_ge(tl["rmul"], at(b, t))
                        pool.nop(nofuse=True)
                        nc.gpsimd.tensor_tensor(x1_t, x1_t, x_in[:, t % 4, :], ALU.add
                                                ).then_inc(tl["resid"], 1)
                    t = s - 1
                    if 0 <= t < NT:
                        inverse_std(2, b, t, "stat3", "z2")

            def split_lo(e, k, n):
                pool.wait_ge(s_whi, n + 1)
                src = w_raw[:, e, :] if isinstance(e, int) else w_raw[:, bass.ds(e, 1), :].rearrange("p a w -> p (a w)")
                pool.nop(nofuse=True)
                nc.gpsimd.tensor_tensor(w_lo[:, k, :], src, w_hi[:, k, :].bitcast(F32), ALU.subtract
                                        ).then_inc(s_wlo, 1)

            def finish(b):
                pool.wait_ge(s_gated, b + 1)
                x1_b = (x1[:, b * BT:(b + 1) * BT, :] if isinstance(b, int)
                        else x1[:, bass.ds(b * BT, BT), :])
                pool.nop(nofuse=True)
                nc.gpsimd.tensor_tensor(y_out, y_out, x1_b, ALU.add).then_inc(s_final, 1)

            def group(b, g, static=False, last=False):
                for k in range(UN):
                    e = g * UN + k + 2
                    if static and e >= EX:
                        if not last:
                            split_lo(e - EX, (k + 2) % UN, b * EX + e)
                    else:
                        split_lo(e, (k + 2) % UN, b * EX + e)

            def rest(b, last=False):
                with pool.Fori(1, NG - 1) as g:
                    group(b, g)
                group(b, NG - 1, static=True, last=last)

            split_lo(0, 0, 0)
            split_lo(1, 1, 1)
            group(0, 0, static=True)
            with pool.Fori(0, NB - 1) as b:
                rest(b)
                group(b + 1, 0, static=True)
                finish(b)
            rest(NB - 1, last=True)
            finish(NB - 1)

        @block.scalar
        def _(act):
            act.dma_start(wmod_sb[:, :, 0:2 * D], wmod[:, 0:2 * D].rearrange("(c p) n -> p c n", p=P)
                          ).then_inc(s_ld_wmod[0], 16)
            act.dma_start(qkv_sb, qkv.rearrange("(c p) n -> p c n", p=P)).then_inc(s_ld_qkv, 16)
            act.dma_start(o_sb, o_proj.rearrange("(c p) n -> p c n", p=P)).then_inc(s_ld_o, 16)
            act.dma_start(wmod_sb[:, :, 4 * D:6 * D], wmod[:, 4 * D:6 * D].rearrange("(c p) n -> p c n", p=P)
                          ).then_inc(s_ld_wmod[2], 16)
            act.wait_ge(s_wr0, 1)
            act.dma_start(wr_raw[:, :, 0:E], w_router.rearrange("(c p) e -> p c e", p=P)).then_inc(s_ld_wr, 16)
            for s in (*act_tile.values(), s_lgT):
                act.sem_inc(s, CREDIT)
            act.wait_ge(s_ld_c, 16 * B)
            nc.scalar.activation(silu_c[:], cols[:, 2:4, :], ACT.Silu).then_inc(s_siluc, 1)

            def load_weights(first, end, sem_):
                for c in range(DC):
                    rows = slice(c * P, (c + 1) * P)
                    act.dma_start(w_raw[:, first:end, W1 + c * P:W1 + (c + 1) * P],
                                  we1[first - SH:end - SH, rows, :].rearrange("e p h -> p e h")).then_inc(sem_, 16)
                    act.dma_start(w_raw[:, first:end, W3 + c * P:W3 + (c + 1) * P],
                                  we3[first - SH:end - SH, rows, :].rearrange("e p h -> p e h")).then_inc(sem_, 16)
                act.dma_start(w_raw[:, first:end, W2:WX],
                              we2[first - SH:end - SH].rearrange("e p d -> p e d")).then_inc(sem_, 16)

            for c in range(DC):
                rows = slice(c * P, (c + 1) * P)
                act.dma_start(w_raw[:, 0:SH, W1 + c * P:W1 + (c + 1) * P],
                              ws1[rows, :].rearrange("p (e h) -> p e h", h=H)).then_inc(s_ld_w, 16)
                act.dma_start(w_raw[:, 0:SH, W3 + c * P:W3 + (c + 1) * P],
                              ws3[rows, :].rearrange("p (e h) -> p e h", h=H)).then_inc(s_ld_w, 16)
            act.dma_start(w_raw[:, 0:SH, W2:WX], ws2.rearrange("(e p) d -> p e d", p=P)).then_inc(s_ld_w, 16)
            load_weights(SH, LATE, s_ld_w)

            act.wait_ge(s_const, 5)
            act.dma_start(cw_dram[0:SH, :], shared_w).then_inc(s_shared, 16)

            act.wait_ge(s_const, 7)
            nc.scalar.activation(ident_r[:], ident[:], ACT.Copy).then_inc(s_constr, 1)
            nc.scalar.activation(mask_r[:], x1[:, 0, 0:P], ACT.Copy).then_inc(s_constr, 1)
            act.wait_ge(s_ld_wr, 16)
            nc.scalar.activation(wr_hi[:], wr_raw, ACT.Copy).then_inc(s_wsp_a, 1)
            act.wait_ge(s_wt_mm, 1)
            nc.scalar.activation(wT_sb[:, 0, :, :], ps[:, 6, :].rearrange("p (k c) -> p k c", k=DC), ACT.Copy
                                 ).then_inc(s_wt_a, 1)
            act.wait_ge(s_wt_mm, 3)
            nc.scalar.activation(wT_sb[:, 2, :, :], ps[:, 5, :].rearrange("p (k c) -> p k c", k=DC), ACT.Copy
                                 ).then_inc(s_wt_a, 1)
            act.wait_ge(s_wqk_mm, 1)
            nc.scalar.activation(wqk_hi, ps[:, 6, :].rearrange("p (c d) -> p c d", c=DC), ACT.Copy,
                                 scale=D ** -0.5).then_inc(s_wsp_a, 1)
            for b in range(B):
                act.wait_ge(s_wvf, b + 1)
                nc.scalar.activation(wvo_hi[:, b, :, :], wT_sb[:, b, :, :], ACT.Copy).then_inc(s_wsp_a, 1)
            act.wait_ge(s_mod_mm, 6)
            act.wait_ge(s_wvo_mm, 1)
            act.wait_ge(s_wsp_d, 4)
            load_weights(LATE, EX, s_ld_w2)
            act.wait_ge(s_shared, 16)

            with act.Fori(0, B) as b:
                for s in range(-2, NT + 2):
                    t = s - 1
                    if 0 <= t < NT:
                        for u, first, n in units_of(t):
                            act.wait_ge(tl["pT"], at_unit(b, u))
                            if u < PT_RING:
                                act.wait_ge(tl["pv"], at(b, -1))
                            else:
                                act.wait_ge(tl["pv"], at(b, tile_of_unit(u - PT_RING)))
                            nc.scalar.activation(pT_hi[:, u % PT_RING, 0:n * P], ps[:, X0 + u % 2, 0:n * P],
                                                 ACT.Copy).then_inc(tl["pthi"], 1)
                    t = s + 2
                    if t < NT:
                        act.wait_ge(tl["xT"], at(b, t))
                        act.wait_ge(s_ld_cols, 32)
                        act.wait_ge(tl["xlo"], at(b, t - 2))
                        for c in range(DC):
                            last = nc.scalar.activation(xf[:, t % 2, c, :], ps[:, Y0, c * P:(c + 1) * P], ACT.Identity,
                                                        scale=cols[:, 0, c:c + 1], bias=cols[:, 1, c:c + 1])
                        last.then_inc(tl["xf"], 1)
                        act.wait_ge(tl["xf"], at(b, t))
                        act.wait_ge(tl["scores"], at(b, -1))
                        nc.scalar.activation(xnT_hi[:, :, t * P:(t + 1) * P], xf[:, t % 2, :, :], ACT.Copy
                                             ).then_inc(tl["xhi"], 1)
                    t = s
                    if 0 <= t < NT:
                        act.wait_ge(tl["negmax"], at(b, t))
                        act.wait_ge(tl["pT"], at_unit(b, units_of(t - 2)[-1][0] if t >= 2 else -1))
                        act.wait_ge(tl["rinv"], at(b, t - 4))
                        if t == 0:
                            act.wait_ge(s_lg_mm, before_row(b))
                        nc.scalar.activation(probs[:, t % 2, 0:(t + 1) * P], score_banks(t), ACT.Exp,
                                             bias=negmax[:, t % 4:t % 4 + 1],
                                             accum_out=rowsum[:, t % 4:t % 4 + 1]).then_inc(tl["exp"], 1)
                    t = s + 1
                    if 0 <= t < NT:
                        act.wait_ge(tl["qv"], at(b, t))
                        act.wait_ge(tl["scores"], at(b, t - 2))
                        nc.scalar.activation(qT_hi[:, t % 2, :, :],
                                             ps[:, Y1, 0:D].rearrange("p (c t) -> p c t", c=DC), ACT.Copy
                                             ).then_inc(tl["qhi"], 1)
                        act.wait_ge(tl["pv"], at(b, -1))
                        nc.scalar.activation(v_hi[:, t, :], ps[:, Y1, D:2 * D], ACT.Copy).then_inc(tl["vhi"], 1)
                    t = s - 2
                    if 0 <= t < NT:
                        act.wait_ge(tl["h2T"], at(b, t))
                        nc.scalar.activation(h2T_hi[:, :, bass.ds(b * S + t * P, P)],
                                             ps[:, Y0, 0:D].rearrange("p (c t) -> p c t", c=DC), ACT.Copy
                                             ).then_inc(tl["hhi"], 1)
                act.wait_ge(s_lgT_mm, at_row(b))
                nc.scalar.activation(logitsT[0:E, :], ps[0:E, 0:2, :].rearrange("p b n -> p (b n)"), ACT.Copy
                                     ).then_inc(s_lgT, 1)

            act.wait_ge(s_rt, R_SHIFTED)
            nc.scalar.activation(expd, expd, ACT.Exp).then_inc(s_rexp, 1)

            def split_hi(e, k, n):
                if not (isinstance(n, int) and n < UN):
                    act.wait_ge(s_y, n - UN + 1)
                src = w_raw[:, e, :] if isinstance(e, int) else w_raw[:, bass.ds(e, 1), :].rearrange("p a w -> p (a w)")
                nc.scalar.activation(w_hi[:, k, :], src, ACT.Copy).then_inc(s_whi, 1)

            def silu_step(k, n):
                act.wait_ge(s_ab, n + 1)
                if not (isinstance(n, int) and n < 2):
                    act.wait_ge(s_glo, n - 2 + 1)
                nc.scalar.activation(act_g[:, k % 2, :], ps[:, 2 * (k % 2), :], ACT.Silu).then_inc(s_silu, 1)

            def g_hi_step(k, n):
                act.wait_ge(s_g, n + 1)
                if not (isinstance(n, int) and n < 2):
                    act.wait_ge(s_y, n - 2 + 1)
                nc.scalar.activation(g_hi[:, k % 2, :], act_g[:, k % 2, :], ACT.Copy).then_inc(s_ghi, 1)

            def evac(b):
                act.wait_ge(s_y, b * EX + EX)
                if not (isinstance(b, int) and b == 0):
                    act.wait_ge(s_yT_mm, b)
                nc.scalar.activation(yT[:, 0, :], ps[:, 4, :], ACT.Copy).then_inc(s_ya, 1)

            def group(b, g, static=False, evac_of=None, last=False):
                for k in range(UN):
                    n = b * EX + (g * UN + k)
                    silu_step(k, n)
                    e = g * UN + k + 2
                    if static and e >= EX:
                        if not last:
                            split_hi(e - EX, (k + 2) % UN, n + 2)
                    else:
                        split_hi(e, (k + 2) % UN, n + 2)
                    if k == 1 and evac_of is not None:
                        evac(evac_of)
                    g_hi_step(k, n)

            def rest(b, last=False):
                with act.Fori(1, NG - 1) as g:
                    group(b, g)
                group(b, NG - 1, static=True, last=last)

            act.wait_ge(s_ld_w, 10 * 16)
            act.wait_ge(tl["scores"], at(B - 1, NT - 1))
            act.wait_ge(tl["pv"], at(B - 1, NT - 1))
            split_hi(0, 0, 0)
            split_hi(1, 1, 1)
            act.wait_ge(s_cwT_mm, 1)
            nc.scalar.activation(cwT[:, 0:2 * BANK], ps[0:E, 4:6, :].rearrange("p b n -> p (b n)"), ACT.Copy
                                 ).then_inc(s_cwT_a, 1)
            act.wait_ge(s_ld_w2, 5 * 16)
            group(0, 0, static=True)
            with act.Fori(0, NB - 1) as b:
                rest(b)
                group(b + 1, 0, static=True, evac_of=b)
            rest(NB - 1, last=True)
            evac(NB - 1)

        @block.vector
        def _(dve):
            for s in (*dve_tile.values(), s_lg):
                dve.sem_inc(s, CREDIT)
            dve.wait_ge(s_siluc, 1)
            dve.wait_ge(s_const, 1)
            for b in range(B):
                for c in range(DC):
                    nc.vector.memset(silu_b[:, b, c, :], 1.0).then_inc(s_silub, 1)
            dve.wait_ge(s_silub, 4)
            for b in range(B):
                for c in range(DC):
                    nc.vector.tensor_scalar(silu_b[:, b, c, :], silu_b[:, b, c, :], silu_c[:, b, c:c + 1], None,
                                            ALU.mult).then_inc(s_silub, 1)
            for b in range(B):
                dve.wait_ge(s_mod_mm, b + 1)
                nc.vector.tensor_copy(mod[:, b, 0:D], ps[:, b, 0:D])
                last = nc.vector.tensor_scalar(mod[:, b, D:2 * D], ps[:, b, D:2 * D], 1.0, None, ALU.add)
            last.then_inc(s_modev, 1)
            dve.wait_ge(s_wsp_a, 1)
            nc.vector.tensor_tensor(wr_lo[:], wr_raw, wr_hi[:].bitcast(F32), ALU.subtract).then_inc(s_wsp_d, 1)
            dve.wait_ge(s_wt_mm, 2)
            nc.vector.tensor_copy(wT_sb[:, 1, :, :], ps[:, 7, :].rearrange("p (k c) -> p k c", k=DC)
                                  ).then_inc(s_wt_d, 1)

            gates = [0]

            def gate(dst, src):
                def then(ins):
                    gates[0] += 1
                    ins.then_inc(s_gt, 1)

                then(nc.vector.tensor_scalar(gate_tmp, src, 0.0, 2.0, ALU.is_ge, ALU.mult))
                then(nc.vector.tensor_copy(dst, src))
                dve.wait_ge(s_gt, gates[0])
                then(nc.vector.scalar_tensor_tensor(out=dst, in0=dst, scalar=-1.0, in1=dst, op0=ALU.mult, op1=ALU.max))
                dve.wait_ge(s_gt, gates[0])
                then(nc.vector.tensor_scalar(dst, dst, GATE_FLOOR, None, ALU.max))
                dve.wait_ge(s_gt, gates[0])
                then(nc.vector.scalar_tensor_tensor(out=dst, in0=gate_tmp, scalar=-1.0, in1=dst, op0=ALU.add,
                                                    op1=ALU.mult))
                dve.wait_ge(s_gt, gates[0])

            for b in range(B):
                dve.wait_ge(s_mod_mm, 3 + b)
                gate(mod[:, b, 2 * D:3 * D], ps[:, 2 + b, 0:D])
                nc.vector.tensor_copy(mod[:, b, 3 * D:4 * D], ps[:, 2 + b, D:2 * D]).then_inc(s_modev, 1)
            dve.wait_ge(s_wqk_mm, 1)
            dve.wait_ge(s_wsp_a, 2)
            nc.vector.scalar_tensor_tensor(out=wqk_lo, in0=ps[:, 6, :].rearrange("p (c d) -> p c d", c=DC),
                                           scalar=D ** -0.5, in1=wqk_hi.bitcast(F32), op0=ALU.mult,
                                           op1=ALU.subtract).then_inc(s_wsp_d, 1)
            dve.wait_ge(s_wvo_mm, 1)
            dve.wait_ge(s_modev, 3)
            for b in range(B):
                for c in range(DC):
                    last = nc.vector.tensor_tensor(wT_sb[:, b, c, :], ps[:, 7, c * D:(c + 1) * D],
                                                   mod[:, b, 2 * D:3 * D], ALU.mult)
                last.then_inc(s_wvf, 1)
            for b in range(B):
                dve.wait_ge(s_wsp_a, 3 + b)
                dve.wait_ge(s_wvf, b + 1)
                nc.vector.tensor_tensor(wvo_lo[:, b, :, :], wT_sb[:, b, :, :], wvo_hi[:, b, :, :].bitcast(F32),
                                        ALU.subtract).then_inc(s_wsp_d, 1)
            for b in range(B):
                dve.wait_ge(s_mod_mm, 5 + b)
                nc.vector.tensor_scalar(mod[:, b, 4 * D:5 * D], ps[:, 4 + b, 0:D], 1.0, None, ALU.add
                                        ).then_inc(s_modev, 1)
                gate(gate_b[:, 2 * b, :], ps[:, 4 + b, D:2 * D])
                nc.vector.tensor_copy(gate_b[:, 2 * b + 1, :], gate_b[:, 2 * b, :]).then_inc(s_modev, 1)

            def normalise(dst, src, which, i):
                return nc.vector.tensor_scalar(dst, src, mv[:, which, i % 4, 0:1], rstd[:, which, i % 4:i % 4 + 1],
                                               ALU.subtract, ALU.mult)

            def stats(src, which, b, i, read_by):
                n = which + 1
                dve.wait_ge(tl[f"stat{n}"], at(b, i - 4))
                dve.nop(nofuse=True)
                nc.vector.bn_stats(bn[:, which, i % 4, :], src).then_inc(tl[f"bn{n}"], 1)
                dve.wait_ge(tl[f"bn{n}"], at(b, i))
                dve.wait_ge(tl[read_by], at(b, i - 4))
                dve.nop(nofuse=True)
                nc.vector.bn_aggr(mv[:, which, i % 4, :], bn[:, which, i % 4, :]).then_inc(tl[f"stat{n}"], 1)

            with dve.Fori(0, B) as b:
                for s in range(-HEADROOM, NT + 2):
                    t = s - 1
                    if 0 <= t < NT:
                        for u, first, n in units_of(t):
                            dve.wait_ge(tl["pthi"], at_unit(b, u))
                            nc.vector.tensor_tensor(pT_lo[:, u % PT_RING, 0:n * P], ps[:, X0 + u % 2, 0:n * P],
                                                    pT_hi[:, u % PT_RING, 0:n * P].bitcast(F32), ALU.subtract
                                                    ).then_inc(tl["ptlo"], 1)
                    t = s + 4
                    if t < NT:
                        dve.wait_ge(s_x[t % 4], b * 32 + (t // 4 + 1) * 16)
                        stats(x_in[:, t % 4, :], 0, b, t, "z")
                    t = s - 2
                    if 0 <= t < NT:
                        dve.wait_ge(tl["rstd3"], at(b, t))
                        dve.wait_ge(tl["h2T"], at(b, t - 2))
                        normalise(h2[:, t % 2, :], x1[:, bass.ds(b * NT + t, 1), :].rearrange("p a d -> p (a d)"),
                                  2, t).then_inc(tl["z2"], 1)
                    t = s
                    if 0 <= t < NT:
                        dve.wait_ge(tl["scores"], at(b, t))
                        dve.wait_ge(tl["exp"], at(b, t - 4))
                        nc.vector.tensor_reduce(negmax[:, t % 4:t % 4 + 1], score_banks(t), AX.X, ALU.max,
                                                negate=True).then_inc(tl["negmax"], 1)
                    t = s + 4
                    if t < NT:
                        dve.wait_ge(tl["rstd1"], at(b, t))
                        dve.wait_ge(tl["xT"], at(b, t - 2))
                        normalise(zx[:, t % 2, :], x_in[:, t % 4, :], 0, t).then_inc(tl["z"], 1)
                    t = s + 2
                    if 0 <= t < NT:
                        dve.wait_ge(tl["xhi"], at(b, t))
                        nc.vector.tensor_tensor(xnT_lo[:, :, t * P:(t + 1) * P], xf[:, t % 2, :, :],
                                                xnT_hi[:, :, t * P:(t + 1) * P].bitcast(F32), ALU.subtract
                                                ).then_inc(tl["xlo"], 1)
                    t = s + 3
                    if 0 <= t < NT:
                        dve.wait_ge(tl["h"], at(b, t))
                        stats(h[:, t % 2, :], 1, b, t, "xn")
                    t = s + 1
                    if 0 <= t < NT:
                        dve.wait_ge(tl["vhi"], at(b, t))
                        nc.vector.tensor_tensor(qT_lo[:, t % 2, :, :],
                                                ps[:, Y1, 0:D].rearrange("p (c t) -> p c t", c=DC),
                                                qT_hi[:, t % 2, :, :].bitcast(F32), ALU.subtract
                                                ).then_inc(tl["qlo"], 1)
                        nc.vector.tensor_tensor(v_lo[:, t, :], ps[:, Y1, D:2 * D], v_hi[:, t, :].bitcast(F32),
                                                ALU.subtract).then_inc(tl["vlo"], 1)
                    t = s + 3
                    if 0 <= t < NT:
                        dve.wait_ge(tl["rstd2"], at(b, t))
                        normalise(zx[:, t % 2, :], h[:, t % 2, :], 1, t).then_inc(tl["xn"], 1)
                    t = s - 2
                    if 0 <= t < NT:
                        dve.wait_ge(tl["hhi"], at(b, t))
                        nc.vector.tensor_tensor(h2T_lo[:, :, bass.ds(b * S + t * P, P)],
                                                ps[:, Y0, 0:D].rearrange("p (c t) -> p c t", c=DC),
                                                h2T_hi[:, :, bass.ds(b * S + t * P, P)].bitcast(F32), ALU.subtract
                                                ).then_inc(tl["hlo"], 1)
                    t = s - 1
                    if 0 <= t < NT:
                        dve.wait_ge(tl["exp"], at(b, t))
                        dve.wait_ge(tl["x1"], at(b, t - 4))
                        nc.vector.reciprocal(rinv[:, t % 4:t % 4 + 1], rowsum[:, t % 4:t % 4 + 1]
                                             ).then_inc(tl["rinv"], 1)
                        dve.wait_ge(tl["rinv"], at(b, t))
                        dve.wait_ge(tl["resid"], at(b, t))
                        dve.wait_ge(tl["pv"], at(b, t))
                        x1_t = x1[:, bass.ds(b * NT + t, 1), :].rearrange("p a d -> p (a d)")
                        nc.vector.scalar_tensor_tensor(out=x1_t, in0=ps[:, Y1, 0:D], scalar=rinv[:, t % 4:t % 4 + 1],
                                                       in1=x1_t, op0=ALU.mult, op1=ALU.add).then_inc(tl["x1"], 1)
                        dve.wait_ge(tl["x1"], at(b, t))
                        stats(x1_t, 2, b, t, "z2")
                dve.wait_ge(s_lg_mm, at_row(b))
                nc.vector.tensor_copy(logits[:, bass.ds(b * NT, NT), :],
                                      ps[:, Y0, 0:NT * E].rearrange("p (t e) -> p t e", e=E)).then_inc(s_lg, 1)

            chain = [0]

            def link(ins):
                chain[0] += 1
                ins.then_inc(s_rt, 1)

            def settle():
                dve.wait_ge(s_rt, chain[0])

            full = (P, B * NT, E)
            dve.wait_ge(s_lg, at_row(B - 1))
            dve.wait_ge(tl["h2"], at(B - 1, NT - 1))
            for t in range(B * NT):
                link(nc.vector.max(top8[:, t, :], logits[:, t, :]))
            settle()
            link(nc.vector.tensor_tensor(expd, logits[:], top8[:, :, 0:1].broadcast_to(full), ALU.subtract))
            assert chain[0] == R_SHIFTED
            link(nc.vector.tensor_tensor(above, logits[:], top8[:, :, TOPK - 1:TOPK].broadcast_to(full), ALU.is_gt))
            link(nc.vector.tensor_tensor(ties, logits[:], top8[:, :, TOPK - 1:TOPK].broadcast_to(full),
                                         ALU.is_equal))
            link(nc.vector.memset(reset, 1.0))
            settle()
            link(nc.vector.memset(reset[:, :, 0:1], 0.0))
            link(nc.vector.tensor_reduce(need, above, AX.X, ALU.add))
            settle()
            link(nc.vector.tensor_scalar(need, need, -1.0, float(TOPK), ALU.mult, ALU.add))
            link(nc.vector.tensor_tensor_scan(nth_tie.rearrange("p t e -> p (t e)"),
                                              reset.rearrange("p t e -> p (t e)"),
                                              ties.rearrange("p t e -> p (t e)"), 0.0, ALU.mult, ALU.add))
            settle()
            link(nc.vector.tensor_tensor(nth_tie, nth_tie, need.broadcast_to(full), ALU.is_le))
            settle()
            link(nc.vector.tensor_tensor(ties, ties, nth_tie, ALU.mult))
            settle()
            link(nc.vector.tensor_tensor(ties, ties, above, ALU.add))
            settle()
            dve.wait_ge(s_rexp, 1)
            link(nc.vector.tensor_tensor(cw, expd, ties, ALU.mult))
            settle()
            link(nc.vector.tensor_reduce(total, cw, AX.X, ALU.add))
            settle()
            link(nc.vector.reciprocal(total, total))
            settle()
            link(nc.vector.tensor_scalar(total, total, TOPK / (TOPK + 1.0), None, ALU.mult))
            settle()
            link(nc.vector.tensor_tensor(cw, cw, total.broadcast_to(full), ALU.mult))
            assert chain[0] == R_DONE
            dve.wait_ge(s_cwT_mm, 1)
            dve.wait_ge(tl["resid"], at(B - 1, NT - 1))
            nc.vector.tensor_copy(cwT[:, 2 * BANK:4 * BANK], ps[0:E, 6:8, :].rearrange("p b n -> p (b n)")
                                  ).then_inc(s_cwT_d, 1)

            def step(k, n, slot_round, between=None):
                dve.wait_ge(s_silu, n + 1)
                nc.vector.tensor_tensor(act_g[:, k % 2, :], act_g[:, k % 2, :], ps[:, 2 * (k % 2) + 1, :],
                                        ALU.mult).then_inc(s_up, 1)
                dve.wait_ge(s_up, n + 1)
                dve.wait_ge(s_cwb[k], slot_round * 16)
                nc.vector.tensor_tensor(act_g[:, k % 2, :], act_g[:, k % 2, :], cwb[:, k, :], ALU.mult
                                        ).then_inc(s_g, 1)
                if between is not None:
                    between()
                dve.wait_ge(s_ghi, n + 1)
                if not (isinstance(n, int) and n < 2):
                    dve.wait_ge(s_y, n - 2 + 1)
                nc.vector.tensor_tensor(g_lo[:, k % 2, :], act_g[:, k % 2, :], g_hi[:, k % 2, :].bitcast(F32),
                                        ALU.subtract).then_inc(s_glo, 1)

            def evac(b):
                dve.wait_ge(s_y, b * EX + EX)
                if not (isinstance(b, int) and b == 0):
                    dve.wait_ge(s_yT_mm, b)
                nc.vector.tensor_copy(yT[:, 1, :], ps[:, 5, :]).then_inc(s_yd, 1)

            def gated(b):
                dve.wait_ge(s_yT_mm, b + 1)
                if not (isinstance(b, int) and b == 0):
                    dve.wait_ge(s_out, b * 16)
                g_b = gate_b[:, b:b + 1, :] if isinstance(b, int) else gate_b[:, bass.ds(b, 1), :]
                nc.vector.tensor_tensor(y_out, ps[:, TR:TR + 2, :].rearrange("p k (t d) -> p (k t) d", d=D),
                                        g_b.broadcast_to((P, BT, D)), ALU.mult).then_inc(s_gated, 1)

            def group(b, g, evac_of=None):
                for k in range(UN):
                    between = (lambda: evac(evac_of)) if k == 1 and evac_of is not None else None
                    step(k, b * EX + (g * UN + k), b * NG + (g + 1), between)

            def rest(b):
                with dve.Fori(1, NG) as g:
                    group(b, g)

            group(0, 0)
            dve.wait_ge(s_cwst, 16)
            with dve.Fori(0, NB - 1) as b:
                rest(b)
                group(b + 1, 0, evac_of=b)
                gated(b)
            rest(NB - 1)
            evac(NB - 1)
            gated(NB - 1)

        @block.tensor
        def _(pe):
            for s in (*pe_tile.values(), s_lgT_mm, s_lg_mm):
                pe.sem_inc(s, CREDIT)

            def split3(dst, w, x_, first, last):
                nc.tensor.matmul(dst, w[0], x_[0], start=first, stop=False)
                nc.tensor.matmul(dst, w[0], x_[1], start=False, stop=False)
                return nc.tensor.matmul(dst, w[1], x_[0], start=False, stop=last)

            def modulation(n, b):
                for c in range(DC):
                    last = nc.tensor.matmul(ps[:, 2 * n + b, :], silu_b[:, b, c, :],
                                            wmod_sb[:, c, n * BANK:(n + 1) * BANK], start=(c == 0), stop=(c == DC - 1))
                last.then_inc(s_mod_mm, 1)

            pe.wait_ge(s_silub, 8)
            pe.wait_ge(s_ld_wmod[0], 16)
            modulation(0, 0)
            modulation(0, 1)
            pe.wait_ge(s_const, 7)
            pe.wait_ge(s_ld_qkv, 16)
            for m, bank in ((0, 6), (1, 7), (2, 5)):
                for k in range(DC):
                    for c in range(DC):
                        last = nc.tensor.transpose(ps[:, bank, k * D + c * P:k * D + (c + 1) * P],
                                                   qkv_sb[:, c, m * D + k * P:m * D + (k + 1) * P], ident[:])
                last.then_inc(s_wt_mm, 1)
            pe.wait_ge(s_ld_wmod[1], 16)
            modulation(1, 0)
            modulation(1, 1)
            pe.wait_ge(s_wt_a, 1)
            pe.wait_ge(s_wt_d, 1)
            for c in range(DC):
                for k in range(DC):
                    last = nc.tensor.matmul(ps[:, 6, c * D:(c + 1) * D], wT_sb[:, 0, k, c * P:(c + 1) * P],
                                            wT_sb[:, 1, k, :], start=(k == 0), stop=(k == DC - 1))
            last.then_inc(s_wqk_mm, 1)
            pe.wait_ge(s_wt_a, 2)
            pe.wait_ge(s_ld_o, 16)
            for c in range(DC):
                for k in range(DC):
                    last = nc.tensor.matmul(ps[:, 7, c * D:(c + 1) * D], wT_sb[:, 2, k, c * P:(c + 1) * P],
                                            o_sb[:, k, :], start=(k == 0), stop=(k == DC - 1))
            last.then_inc(s_wvo_mm, 1)
            pe.wait_ge(s_ld_wmod[2], 16)
            modulation(2, 0)
            modulation(2, 1)

            pe.wait_ge(s_constr, 2)
            pe.wait_ge(s_wsp_d, 4)
            pe.wait_ge(s_modev, 7)
            with pe.Fori(0, B) as b:
                for s in range(-2, NT + 2):
                    t = s - 1
                    if 0 <= t < NT:
                        pe.wait_ge(tl["exp"], at(b, t))
                        for u, first, n in units_of(t):
                            pe.wait_ge(tl["ptlo"], at_unit(b, u - 2))
                            for j in range(n):
                                last = nc.tensor.transpose(ps[:, X0 + u % 2, j * P:(j + 1) * P],
                                                           probs[:, t % 2, (first + j) * P:(first + j + 1) * P],
                                                           ident[:])
                            last.then_inc(tl["pT"], 1)
                    t = s
                    if 0 <= t < NT:
                        pe.wait_ge(tl["qlo"], at(b, t))
                        pe.wait_ge(tl["xlo"], at(b, t))
                        pe.wait_ge(tl["exp"], at(b, t - 2))
                        for first in range(0, t + 1, BT):
                            end = min(first + BT, t + 1)
                            dst = ps[:, 2 * (t % 2) + first // BT, 0:(end - first) * P]
                            keys = slice(first * P, end * P)
                            own = end == t + 1
                            for c in range(DC):
                                last = split3(dst, (qT_hi[:, t % 2, c, :], qT_lo[:, t % 2, c, :]),
                                              (xnT_hi[:, c, keys], xnT_lo[:, c, keys]), c == 0,
                                              c == DC - 1 and not own)
                            if own:
                                last = nc.tensor.matmul(dst[:, (end - first - 1) * P:(end - first) * P], ident_r[:],
                                                        mask_r[:], start=False, stop=True)
                        last.then_inc(tl["scores"], 1)
                    t = s + 2
                    if t < NT:
                        pe.wait_ge(tl["xn"], at(b, t))
                        if t == 0:
                            pe.wait_ge(s_lg, before_row(b))
                        pe.wait_ge(tl["xf"], at(b, t - 1))
                        pe.wait_ge(tl["hlo"], at(b, max(t - 5, -1)))
                        for c in range(DC):
                            last = nc.tensor.transpose(ps[:, Y0, c * P:(c + 1) * P], zx[:, t % 2, c * P:(c + 1) * P],
                                                       ident[:])
                        last.then_inc(tl["xT"], 1)
                    t = s + 1
                    if 0 <= t < NT:
                        pe.wait_ge(tl["xlo"], at(b, t))
                        pe.wait_ge(tl["x1"], at(b, max(t - 3, -1)))
                        pe.wait_ge(tl["vlo"], at(b, t - 1))
                        tok = slice(t * P, (t + 1) * P)
                        for m in range(DC):
                            for c in range(DC):
                                split3(ps[:, Y1, m * P:(m + 1) * P],
                                       (wqk_hi[:, c, m * P:(m + 1) * P], wqk_lo[:, c, m * P:(m + 1) * P]),
                                       (xnT_hi[:, c, tok], xnT_lo[:, c, tok]), c == 0, c == DC - 1)
                        for c in range(DC):
                            w_b = [w[:, bass.ds(b, 1), c, :].rearrange("p a d -> p (a d)") for w in (wvo_hi, wvo_lo)]
                            last = split3(ps[:, Y1, D:2 * D], (xnT_hi[:, c, tok], xnT_lo[:, c, tok]), w_b,
                                          c == 0, c == DC - 1)
                        last.then_inc(tl["qv"], 1)
                    t = s - 2
                    if 0 <= t < NT:
                        pe.wait_ge(tl["h2"], at(b, t))
                        pe.wait_ge(tl["xf"], at(b, min(t + 4, NT - 1)))
                        pe.wait_ge(tl["hlo"], at(b, t - 1))
                        for c in range(DC):
                            last = nc.tensor.transpose(ps[:, Y0, c * P:(c + 1) * P], h2[:, t % 2, c * P:(c + 1) * P],
                                                       ident[:])
                        last.then_inc(tl["h2T"], 1)
                    t = s - 1
                    if 0 <= t < NT:
                        pe.wait_ge(tl["vlo"], at(b, min(t + 2, NT - 1)))
                        pe.wait_ge(tl["x1"], at(b, t - 1))
                        for u, first, n in units_of(t):
                            pe.wait_ge(tl["ptlo"], at_unit(b, u))
                            for j in range(n):
                                last = split3(ps[:, Y1, 0:D],
                                              [m[:, u % PT_RING, j * P:(j + 1) * P] for m in (pT_hi, pT_lo)],
                                              [m[:, first + j, :] for m in (v_hi, v_lo)],
                                              first + j == 0, first + j == t)
                        last.then_inc(tl["pv"], 1)
                pe.wait_ge(tl["hlo"], at(b, NT - 1))
                pe.wait_ge(tl["exp"], at(b, NT - 2))
                for half in range(S // TB):
                    tok = bass.ds(b * S + half * TB, TB)
                    for c in range(DC):
                        last = split3(ps[:, half, :], (wr_hi[:, c, :], wr_lo[:, c, :]),
                                      (h2T_hi[:, c, tok], h2T_lo[:, c, tok]), c == 0, c == DC - 1)
                last.then_inc(s_lgT_mm, 1)
                pe.wait_ge(s_lgT, at_row(b))
                pe.nop(nofuse=True)
                for t in range(NT):
                    last = nc.tensor.transpose(ps[:, Y0, t * E:(t + 1) * E], logitsT[0:E, t * P:(t + 1) * P],
                                               ident[0:E, 0:E])
                last.then_inc(s_lg_mm, 1)

            def gate_up(b, k, n):
                pe.wait_ge(s_wlo, n + 1)
                if not (isinstance(n, int) and n < 2):
                    pe.wait_ge(s_up, n - 2 + 1)
                tok = slice(b * TB, (b + 1) * TB) if isinstance(b, int) else bass.ds(b * TB, TB)
                for bank, at_ in ((2 * (k % 2), W1), (2 * (k % 2) + 1, W3)):
                    for c in range(DC):
                        cols_ = slice(at_ + c * P, at_ + (c + 1) * P)
                        last = split3(ps[:, bank, :], (w_hi[:, k, cols_], w_lo[:, k, cols_]),
                                      (h2T_hi[:, c, tok], h2T_lo[:, c, tok]), c == 0, c == DC - 1)
                last.then_inc(s_ab, 1)

            def down(k, n, first=False, final=False, drained=None):
                pe.wait_ge(s_glo, n + 1)
                if drained is not None:
                    pe.wait_ge(s_ya, drained)
                    pe.wait_ge(s_yd, drained)
                for c in range(DC):
                    cols_ = slice(W2 + c * P, W2 + (c + 1) * P)
                    last = split3(ps[:, 4 + c, :], (w_hi[:, k, cols_], w_lo[:, k, cols_]),
                                  (g_hi[:, k % 2, :], g_lo[:, k % 2, :]), first, final)
                last.then_inc(s_y, 1)

            def turn_back(b):
                pe.wait_ge(s_ya, b + 1)
                pe.wait_ge(s_yd, b + 1)
                if not (isinstance(b, int) and b == 0):
                    pe.wait_ge(s_gated, b)
                for j in range(BT):
                    for c in range(DC):
                        last = nc.tensor.transpose(
                            ps[:, TR + j // 2, (j % 2) * D + c * P:(j % 2) * D + (c + 1) * P],
                            yT[:, c, j * P:(j + 1) * P], ident[:])
                last.then_inc(s_yT_mm, 1)

            def head(b, before=None):
                for k in range(UN):
                    n = b * EX + k
                    gate_up(b, k, n)
                    if k == 0 and before is None:
                        cw_rows()
                    if k >= 2:
                        down(k - 2, n - 2, first=(k == 2), drained=None if before is None else before + 1)
                    elif before is not None:
                        down(k + 2, n - 2, final=(k == 1))
                if before is not None:
                    turn_back(before)

            def cw_rows():
                pe.wait_ge(s_rt, R_DONE)
                for t in range(B * NT):
                    last = nc.tensor.transpose(ps[0:E, 4 + t // BT, (t % BT) * P:(t % BT + 1) * P], cw[:, t, :],
                                               ident[:])
                last.then_inc(s_cwT_mm, 1)
                pe.wait_ge(s_cwT_a, 1)
                pe.wait_ge(s_cwT_d, 1)

            def rest(b):
                with pe.Fori(1, NG) as g:
                    for k in range(UN):
                        n = b * EX + (g * UN + k)
                        gate_up(b, k, n)
                        down((k + 2) % UN, n - 2)

            head(0)
            with pe.Fori(0, NB - 1) as b:
                rest(b)
                head(b + 1, before=b)
            rest(NB - 1)
            down(2, T // TB * EX - 2)
            down(3, T // TB * EX - 1, final=True)
            turn_back(NB - 1)


def tile_of_unit(u):
    return u if u < BT else BT + (u - BT) // 2


_INS = ['L0_attn_x', 'L0_attn_qkv', 'L0_attn_o_proj', 'L0_attn_gamma', 'L0_attn_beta', 'L0_ffn_w_router',
        'L0_ffn_we1', 'L0_ffn_we3', 'L0_ffn_we2', 'L0_ffn_ws1', 'L0_ffn_ws3', 'L0_ffn_ws2', 'L0_c', 'L0_wmod']
_OUTS = [((B, S, D), 'float32')]


def kernel(**inputs):
    import numpy as _np
    import concourse.bacc as _bacc
    from concourse import mybir as _mybir
    from concourse.bass_utils import run_bass_kernel_spmd as _run

    nc = _bacc.Bacc("TRN2", target_bir_lowering=False, num_devices=1)
    arrays, args = {}, []
    for name in _INS:
        a = _np.ascontiguousarray(inputs[name])
        arrays[f"in_{name}_dram"] = a
        args.append(nc.dram_tensor(f"in_{name}_dram", a.shape, _mybir.dt.from_np(a.dtype), kind="ExternalInput").ap())
    for i, (shape, dtype) in enumerate(_OUTS):
        dt = _mybir.dt.from_np(_np.dtype(dtype))
        args.append(nc.dram_tensor(f"out_{i}_dram", shape, dt, kind="ExternalOutput").ap())
    adaln_block(nc, *args)
    r = _run(nc, [arrays], core_ids=[0])
    return r.results[0]["out_0_dram"]
```

```python
from contextlib import ExitStack

import concourse.bass as bass
from concourse import mybir

F32 = mybir.dt.float32
F32R = mybir.dt.float32r
ALU = mybir.AluOpType
ACT = mybir.ActivationFunctionType
AX = mybir.AxisListType

P = 128
D = 256
DC = D // P
B, S = 2, 1024
T = B * S
NT = S // P
TILES = B * NT
E = 16
TOPK = 4
H = 128
HS = 512
SH = HS // H
EX = SH + E
TB = 512
NB = T // TB
BT = TB // P
EPS = 1e-5
BANK = 512
MASKED = -1e30
GATE_FLOOR = 0.25

W1, W3, W2, WX = 0, D, 2 * D, 3 * D
UN = 4
NG = EX // UN
FIRST = -5
LAST = TILES
KEY_SLOTS = NT + 2
SPLIT_MM = 3
EARLY, MID = 11, 16


def slot_of(t):
    return t if t < KEY_SLOTS else t - KEY_SLOTS


def key_runs(first, end):
    runs = []
    for t in range(first, end):
        if runs and slot_of(t) == runs[-1][1] + runs[-1][2]:
            runs[-1][2] += 1
        else:
            runs.append([t - first, slot_of(t), 1])
    return runs


def units_of(t):
    row, i = divmod(t, NT)
    first = row * UNITS + (i if i < BT else BT + 2 * (i - BT))
    return [(first + n // BT, n, min(BT, i + 1 - n)) for n in range(0, i + 1, BT)]


UNITS = BT + 2 * (NT - BT)
PT_RING = 3
ROUTE = NT + 3


def tile_of_unit(u):
    row, v = divmod(u, UNITS)
    return row * NT + (v if v < BT else BT + (v - BT) // 2)


R_SHIFTED = NT + 1
R_ROW = R_SHIFTED + 15


def adaln_block(nc, x, qkv, o_proj, gamma, beta, w_router, we1, we3, we2, ws1, ws3, ws2, c_in, wmod, out):
    cw_dram = nc.dram_tensor("cw_rows", (EX, T), F32, kind="Internal").ap()
    ctx = ExitStack()
    with ctx:
        def sb(name, shape, dt=F32):
            return ctx.enter_context(nc.sbuf_tensor(name, shape, dt))

        def sem(name):
            return ctx.enter_context(nc.semaphore(name))

        w_raw = sb("w_raw", [P, EX, WX])
        h2T_hi = sb("h2T_hi", [P, DC, T], F32R)
        h2T_lo = sb("h2T_lo", [P, DC, T], F32R)
        x1 = sb("x1", [P, B * NT, D])
        mod = sb("mod", [P, B, 3 * D])
        mod_cols = sb("mod_cols", [P, B, 2, DC])
        gate_b = sb("gate_b", [P, NB, D])
        ident = sb("ident", [P, P])
        ident_r = sb("ident_r", [P, P], F32R)
        mask_r = sb("mask_r", [P, P], F32R)
        wr_hi = sb("wr_hi", [P, DC, P], F32R)
        wr_lo = sb("wr_lo", [P, DC, P], F32R)
        logits = sb("logits", [P, TILES, E])
        cols = sb("cols", [P, 4, DC])
        silu_c = sb("silu_c", [P, B, DC])
        minus_half = sb("minus_half", [P, 1])
        eps = sb("eps", [P, 1])
        bn = sb("bn", [P, 3, 4, 6])
        mv = sb("mv", [P, 3, 4, 2])
        veps = sb("veps", [P, 3, 4])
        rstd = sb("rstd", [P, 3, 4])
        shift = sb("shift", [P, 3, 4])
        negmax = sb("negmax", [P, 4])
        rowsum = sb("rowsum", [P, 4])
        rinv = sb("rinv", [P, 4])

        rpool = sb("rpool", [P, 17408], F32R)

        def r_part(at, n):
            return rpool[:, at:at + n]

        KS = KEY_SLOTS * P
        V_HI, Q_HI, V_LO, Q_LO = 0, KEY_SLOTS * D, KEY_SLOTS * D + 2 * D, 2 * KEY_SLOTS * D + 2 * D
        v_hi = r_part(V_HI, KEY_SLOTS * D).rearrange("p (t d) -> p t d", d=D)
        v_lo = r_part(V_LO, KEY_SLOTS * D).rearrange("p (t d) -> p t d", d=D)
        qT_hi = r_part(Q_HI, 2 * D).rearrange("p (s c t) -> p s c t", s=2, c=DC)
        qT_lo = r_part(Q_LO, 2 * D).rearrange("p (s c t) -> p s c t", s=2, c=DC)
        xnT_hi = r_part(6144, DC * KS).rearrange("p (c t) -> p c t", c=DC)
        xnT_lo = r_part(8704, DC * KS).rearrange("p (c t) -> p c t", c=DC)
        pT_hi = r_part(11264, 1536).rearrange("p (u k) -> p u k", k=BANK)
        pT_lo = r_part(12800, 1536).rearrange("p (u k) -> p u k", k=BANK)
        wqk_hi = r_part(14336, 512).rearrange("p (c d) -> p c d", c=DC)
        wqk_lo = r_part(14848, 512).rearrange("p (c d) -> p c d", c=DC)
        wvo_hi = r_part(15360, 1024).rearrange("p (b c d) -> p b c d", b=B, c=DC)
        wvo_lo = r_part(16384, 1024).rearrange("p (b c d) -> p b c d", b=B, c=DC)

        def vq(v0, q0, t):
            at = v0 + slot_of(t) * D
            apart = q0 + t % 2 * D - at
            return r_part(at, 2 * apart).rearrange("p (two x) -> p two x", two=2)[:, :, 0:D]

        slots = [14336, 14336 + 2 * WX, 6144, 6144 + 2 * WX]
        w_hi = [r_part(at, WX) for at in slots]
        w_lo = [r_part(at + WX, WX) for at in slots]
        g_hi = r_part(0, 2 * TB).rearrange("p (s t) -> p s t", s=2)
        g_lo = r_part(2 * TB, 2 * TB).rearrange("p (s t) -> p s t", s=2)

        fpool = sb("fpool", [P, 4096])

        def f_part(at, n):
            return fpool[:, at:at + n]

        x_in = f_part(0, 1024).rearrange("p (s d) -> p s d", s=4)
        h = f_part(1024, 512).rearrange("p (s d) -> p s d", s=2)
        xn = f_part(1536, 512).rearrange("p (s d) -> p s d", s=2)
        logitsT = fpool[0:E, 2048:2048 + S]
        cwT = logitsT
        xf = f_part(3072, 512).rearrange("p (s c t) -> p s c t", s=2, c=DC)
        z2 = f_part(3584, 512).rearrange("p (s d) -> p s d", s=2)
        act_g = f_part(0, 2 * TB).rearrange("p (s t) -> p s t", s=2)
        cwb = f_part(1024, 2 * TB).rearrange("p (s t) -> p s t", s=2)
        yT = f_part(2048, DC * TB).rearrange("p (c t) -> p c t", c=DC)
        y_out = f_part(3072, BT * D).rearrange("p (t d) -> p t d", t=BT)
        gate_tmp = f_part(1536, D)
        silu_b = f_part(3584, 512).rearrange("p (b c q) -> p b c q", b=B, c=DC)
        wr_raw = f_part(2048, DC * P).rearrange("p (c e) -> p c e", c=DC)
        mask_raw = f_part(3072, P)
        shared_row = sb("shared_row", [SH, P])
        stage = w_raw[:, EARLY:EX, :].rearrange("p e w -> p (e w)")
        qkv_sb = stage[:, 0:1536].rearrange("p (c n) -> p c n", c=DC)
        o_sb = stage[:, 1536:2048].rearrange("p (c n) -> p c n", c=DC)
        wT_sb = stage[:, 2048:3584].rearrange("p (m k c) -> p m k c", m=3, k=DC)
        wmod_sb = stage[:, 3584:6656].rearrange("p (c n) -> p c n", c=DC)
        probs = stage[:, 0:2048].rearrange("p (s k) -> p s k", s=2)
        h2f = stage[:, 2048:2560].rearrange("p (s c t) -> p s c t", s=2, c=DC)
        rt = mod[:, 0, :]
        top8 = rt[:, 0:64].rearrange("p (t k) -> p t k", k=8)
        above = rt[:, 64:192].rearrange("p (t e) -> p t e", e=E)
        ties = rt[:, 192:320].rearrange("p (t e) -> p t e", e=E)
        nth_tie = rt[:, 320:448].rearrange("p (t e) -> p t e", e=E)
        cw = rt[:, 448:576].rearrange("p (t e) -> p t e", e=E)
        reset = rt[:, 576:704].rearrange("p (t e) -> p t e", e=E)
        need = rt[:, 704:712].rearrange("p (t e) -> p t e", e=1)
        total = rt[:, 712:720].rearrange("p (t e) -> p t e", e=1)

        ps = ctx.enter_context(nc.psum_tensor("ps", [P, 8, BANK], F32))
        X0, Y0, Y1, TR = 4, 6, 7, 6

        def score_banks(t):
            return ps[:, 2 * (t % 2):2 * (t % 2) + 2, :].rearrange("p b n -> p (b n)")[:, 0:(t % NT + 1) * P]

        s_ld_c, s_ld_cols, s_ld_qkv, s_ld_o, s_ld_wr = (sem(n) for n in (
            "ld_c", "ld_cols", "ld_qkv", "ld_o", "ld_wr"))
        s_ld_wmod = [sem(f"ld_wmod{n}") for n in range(3)]
        s_ld_w = sem("ld_w_early")
        s_ld_w2 = sem("ld_w_last")
        s_ld_w3 = sem("ld_w_middle")
        s_x = [sem(f"x_loaded{n}") for n in range(4)]
        s_cwb = [sem(f"weights_bcast{n}") for n in range(2)]
        s_shared = sem("shared_rows_stored")
        s_cwst = sem("cw_rows_stored")
        s_out = sem("out_stored")
        s_const, s_siluc, s_silub, s_mod_mm, s_modev, s_gt, s_wt_mm, s_wt_a, s_wt_d = (sem(n) for n in (
            "const", "siluc", "silub", "mod_mm", "mod_evac", "gate_chain", "wT_mm", "wT_act", "wT_dve"))
        s_wr0 = sem("router_pad_zeroed")
        s_constr, s_wqk_mm, s_wvo_mm, s_wsp_a, s_wsp_d, s_wvf = (sem(n) for n in (
            "const_r", "wqk_mm", "wvo_mm", "wsplit_hi", "wsplit_lo", "wvo_gated"))
        tl = {n: sem("t_" + n) for n in (
            "bn1", "stat1", "u", "h", "bn2", "stat2", "xlo", "negmax", "vqlo", "ptlo", "rinv", "x1", "bn3", "stat3",
            "hlo",
            "eps1", "rstd1", "eps2", "rstd2", "shift2", "rmul", "resid", "eps3", "rstd3", "shift3", "z2",
            "xT", "vq", "scores", "pT", "h2T", "pv",
            "xn", "xf", "xhi", "exp", "vqhi", "pthi", "h2f", "hhi")}

        def done(eng, stage_, t):
            if t >= 0:
                eng.wait_ge(tl[stage_], t + 1)

        s_lgT_mm, s_lgT, s_lg_mm, s_lg = (sem(n) for n in ("logitsT_mm", "logitsT", "logits_mm", "logits_evac"))
        s_rt, s_rexp, s_cwT_mm, s_cwT = (sem(n) for n in ("router_chain", "router_exp", "cwT_mm", "cwT_evac"))
        s_whi, s_wlo, s_ab, s_y, s_silu, s_up, s_g, s_ghi, s_glo = (sem(n) for n in (
            "w_hi", "w_lo", "gate_up_mm", "down_mm", "silu", "up_mul", "g", "g_hi", "g_lo"))
        s_ya, s_yd, s_yT_mm, s_gated, s_final = (sem(n) for n in (
            "y_evac_act", "y_evac_dve", "y_back", "y_gated", "y_final"))

        x_t = x.rearrange("b (i p) d -> b i p d", p=P)
        out_t = out.rearrange("b (n t p) d -> (b n) p t d", t=BT, p=P)

        def load_weights(eng, first, end, sem_):
            for c in range(DC):
                rows = slice(c * P, (c + 1) * P)
                for w, at in ((we1, W1), (we3, W3)):
                    eng.dma_start(w_raw[:, first:end, at + c * P:at + (c + 1) * P],
                                  w[first - SH:end - SH, rows, :].rearrange("e p h -> p e h")).then_inc(sem_, 16)
            eng.dma_start(w_raw[:, first:end, W2:WX],
                          we2[first - SH:end - SH].rearrange("e p d -> p e d")).then_inc(sem_, 16)

        block = ctx.enter_context(nc.Block())

        @block.sync
        def _(sp):
            with nc.allow_non_contiguous_dma(reason="small column loads"):
                for b in range(B):
                    sp.dma_start(cols[:, 2 + b, :], c_in[b].rearrange("(c p) -> p c", p=P)).then_inc(s_ld_c, 16)
                sp.dma_start(cols[:, 0, :], gamma.rearrange("(c p) -> p c", p=P)).then_inc(s_ld_cols, 16)
                sp.dma_start(cols[:, 1, :], beta.rearrange("(c p) -> p c", p=P)).then_inc(s_ld_cols, 16)
            sp.dma_start(wmod_sb[:, :, 2 * D:4 * D], wmod[:, 2 * D:4 * D].rearrange("(c p) n -> p c n", p=P)
                         ).then_inc(s_ld_wmod[1], 16)
            for t in range(TILES):
                done(sp, "resid", t - 4)
                sp.dma_start(x_in[:, t % 4, :], x_t[t // NT, t % NT]).then_inc(s_x[t % 4], 16)

            def weights(b, e, k, n):
                if not (isinstance(n, int) and n < 2):
                    sp.wait_ge(s_g, n - 2 + 1)
                row = cw_dram[e:e + 1, :] if isinstance(e, int) else cw_dram[bass.ds(e, 1), :]
                cut = row[:, b * TB:(b + 1) * TB] if isinstance(b, int) else row[:, bass.ds(b * TB, TB)]
                sp.dma_start(cwb[:, k % 2, :], cut.broadcast_to((P, TB))).then_inc(s_cwb[k % 2], 16)

            def store(b):
                sp.wait_ge(s_final, b + 1)
                dst = out_t[b] if isinstance(b, int) else out_t[bass.ds(b, 1)].rearrange("a p t d -> (a p) t d")
                sp.dma_start(dst, y_out).then_inc(s_out, 16)

            def group(b, g):
                for k in range(UN):
                    e = g * UN + k
                    weights(b, e, k, b * EX + e)

            sp.wait_ge(s_shared, 16)
            done(sp, "resid", TILES - 1)
            done(sp, "xT", TILES - 1)
            group(0, 0)
            done(sp, "pT", B * UNITS - 1)
            done(sp, "hlo", TILES - 1)
            load_weights(sp, EARLY, MID, s_ld_w3)
            sp.wait_ge(s_cwT, 1)
            sp.dma_start(cw_dram[SH:EX, 0:S], cwT).then_inc(s_cwst, 16)
            sp.wait_ge(s_cwst, 16)
            group(0, 1)
            sp.wait_ge(s_cwT, 2)
            sp.dma_start(cw_dram[SH:EX, S:T], cwT).then_inc(s_cwst, 16)
            with sp.Fori(2, NG) as g:
                group(0, g)
            sp.wait_ge(s_cwst, 32)
            with sp.Fori(1, NB) as b:
                group(b, 0)
                group(b, 1)
                store(b - 1)
                with sp.Fori(2, NG) as g:
                    group(b, g)
            store(NB - 1)
            sp.wait_ge(s_out, 16 * NB)

        @block.gpsimd
        def _(pool):
            nc.gpsimd.memset(ident[:], 1.0).then_inc(s_const, 1)
            nc.gpsimd.memset(mask_raw, 0.0).then_inc(s_const, 1)
            nc.gpsimd.memset(eps[:], EPS).then_inc(s_const, 1)
            nc.gpsimd.memset(minus_half[:], -0.5).then_inc(s_const, 1)
            nc.gpsimd.memset(shared_row[:], 1.0 / (TOPK + 1)).then_inc(s_const, 1)
            nc.gpsimd.memset(wr_raw, 0.0).then_inc(s_wr0, 1)
            pool.wait_ge(s_const, 5)
            nc.gpsimd.affine_select(out=ident[:], in_=ident[:], compare_op=ALU.is_equal, fill=0.0, base=0,
                                    pattern=[[-1, P]], channel_multiplier=1).then_inc(s_const, 1)
            nc.gpsimd.affine_select(out=mask_raw, in_=mask_raw, compare_op=ALU.is_ge, fill=MASKED,
                                    base=0, pattern=[[-1, P]], channel_multiplier=1).then_inc(s_const, 1)

            def inverse_std(n, t, read_by):
                v, r = veps[:, n - 1, t % 4:t % 4 + 1], rstd[:, n - 1, t % 4:t % 4 + 1]
                done(pool, f"stat{n}", t)
                nc.gpsimd.tensor_tensor(v, mv[:, n - 1, t % 4, 1:2], eps[:], ALU.add).then_inc(tl[f"eps{n}"], 1)
                done(pool, f"eps{n}", t)
                done(pool, read_by, t - 4)
                nc.gpsimd.tensor_tensor(r, v, minus_half[:], ALU.pow).then_inc(tl[f"rstd{n}"], 1)

            def mean_shift(n, t):
                done(pool, f"rstd{n}", t)
                nc.gpsimd.tensor_scalar(shift[:, n - 1, t % 4:t % 4 + 1], mv[:, n - 1, t % 4, 0:1],
                                        rstd[:, n - 1, t % 4:t % 4 + 1], -1.0, ALU.mult, ALU.mult
                                        ).then_inc(tl[f"shift{n}"], 1)

            def norm2(t):
                inverse_std(3, t, "z2")
                mean_shift(3, t)
                done(pool, "shift3", t)
                done(pool, "h2T", t - 2)
                nc.gpsimd.tensor_scalar(z2[:, t % 2, :], x1[:, t, :], rstd[:, 2, t % 4:t % 4 + 1],
                                        shift[:, 2, t % 4:t % 4 + 1], ALU.mult, ALU.add).then_inc(tl["z2"], 1)

            for s in range(FIRST, LAST + 1):
                if 0 <= s - 2:
                    norm2(s - 2)
                if s + 5 < TILES:
                    inverse_std(1, s + 5, "h")
                t = s + 3
                if 0 <= t < TILES:
                    done(pool, "h", t)
                    if t == 0:
                        pool.wait_ge(s_modev, 3)
                    nc.gpsimd.tensor_tensor(x1[:, t, :], h[:, t % 2, :], mod[:, t // NT, 2 * D:3 * D], ALU.mult
                                            ).then_inc(tl["rmul"], 1)
                    done(pool, "rmul", t)
                    nc.gpsimd.tensor_tensor(x1[:, t, :], x1[:, t, :], x_in[:, t % 4, :], ALU.add
                                            ).then_inc(tl["resid"], 1)
                t = s + 4
                if 0 <= t < TILES:
                    inverse_std(2, t, "xn")
                    mean_shift(2, t)
            norm2(TILES - 1)

            def split_lo(e, k, n):
                pool.wait_ge(s_whi, n + 1)
                src = w_raw[:, e, :] if isinstance(e, int) else w_raw[:, bass.ds(e, 1), :].rearrange("p a w -> p (a w)")
                pool.nop(nofuse=True)
                nc.gpsimd.tensor_tensor(w_lo[k], src, w_hi[k].bitcast(F32), ALU.subtract
                                        ).then_inc(s_wlo, 1)

            def finish(b):
                pool.wait_ge(s_gated, b + 1)
                x1_b = (x1[:, b * BT:(b + 1) * BT, :] if isinstance(b, int)
                        else x1[:, bass.ds(b * BT, BT), :])
                pool.nop(nofuse=True)
                nc.gpsimd.tensor_tensor(y_out, y_out, x1_b, ALU.add).then_inc(s_final, 1)

            def group(b, g, static=False, last=False):
                for k in range(UN):
                    e = g * UN + k + 2
                    if static and e >= EX:
                        if not last:
                            split_lo(e - EX, (k + 2) % UN, b * EX + e)
                    else:
                        split_lo(e, (k + 2) % UN, b * EX + e)

            def rest(b, first=1, last=False):
                with pool.Fori(first, NG - 1) as g:
                    group(b, g)
                group(b, NG - 1, static=True, last=last)

            split_lo(0, 0, 0)
            split_lo(1, 1, 1)
            group(0, 0, static=True)
            group(0, 1, static=True)
            rest(0, first=2)
            group(1, 0, static=True)
            finish(0)
            with pool.Fori(1, NB - 1) as b:
                rest(b)
                group(b + 1, 0, static=True)
                finish(b)
            rest(NB - 1, last=True)
            finish(NB - 1)

        @block.scalar
        def _(act):
            act.dma_start(wmod_sb[:, :, 0:2 * D], wmod[:, 0:2 * D].rearrange("(c p) n -> p c n", p=P)
                          ).then_inc(s_ld_wmod[0], 16)
            act.dma_start(qkv_sb, qkv.rearrange("(c p) n -> p c n", p=P)).then_inc(s_ld_qkv, 16)
            act.dma_start(o_sb, o_proj.rearrange("(c p) n -> p c n", p=P)).then_inc(s_ld_o, 16)
            act.dma_start(wmod_sb[:, :, 4 * D:6 * D], wmod[:, 4 * D:6 * D].rearrange("(c p) n -> p c n", p=P)
                          ).then_inc(s_ld_wmod[2], 16)
            act.wait_ge(s_wr0, 1)
            act.dma_start(wr_raw[:, :, 0:E], w_router.rearrange("(c p) e -> p c e", p=P)).then_inc(s_ld_wr, 16)
            act.wait_ge(s_ld_c, 16 * B)
            nc.scalar.activation(silu_c[:], cols[:, 2:4, :], ACT.Silu).then_inc(s_siluc, 1)

            for c in range(DC):
                rows = slice(c * P, (c + 1) * P)
                act.dma_start(w_raw[:, 0:SH, W1 + c * P:W1 + (c + 1) * P],
                              ws1[rows, :].rearrange("p (e h) -> p e h", h=H)).then_inc(s_ld_w, 16)
                act.dma_start(w_raw[:, 0:SH, W3 + c * P:W3 + (c + 1) * P],
                              ws3[rows, :].rearrange("p (e h) -> p e h", h=H)).then_inc(s_ld_w, 16)
            act.dma_start(w_raw[:, 0:SH, W2:WX], ws2.rearrange("(e p) d -> p e d", p=P)).then_inc(s_ld_w, 16)
            load_weights(act, SH, EARLY, s_ld_w)

            act.wait_ge(s_const, 5)
            act.dma_start(cw_dram[0:SH, :].rearrange("e (n t) -> e n t", t=P),
                          shared_row[:].rearrange("e (n t) -> e n t", n=1).broadcast_to((SH, T // P, P))
                          ).then_inc(s_shared, 16)

            act.wait_ge(s_const, 7)
            nc.scalar.activation(ident_r[:], ident[:], ACT.Copy).then_inc(s_constr, 1)
            nc.scalar.activation(mask_r[:], mask_raw, ACT.Copy).then_inc(s_constr, 1)
            act.wait_ge(s_ld_wr, 16)
            nc.scalar.activation(wr_hi[:], wr_raw, ACT.Copy).then_inc(s_wsp_a, 1)
            act.wait_ge(s_wt_mm, 1)
            nc.scalar.activation(wT_sb[:, 0, :, :], ps[:, 6, :].rearrange("p (k c) -> p k c", k=DC), ACT.Copy
                                 ).then_inc(s_wt_a, 1)
            act.wait_ge(s_wt_mm, 3)
            nc.scalar.activation(wT_sb[:, 2, :, :], ps[:, 5, :].rearrange("p (k c) -> p k c", k=DC), ACT.Copy
                                 ).then_inc(s_wt_a, 1)
            act.wait_ge(s_wqk_mm, 1)
            nc.scalar.activation(wqk_hi, ps[:, 6, :].rearrange("p (c d) -> p c d", c=DC), ACT.Copy,
                                 scale=D ** -0.5).then_inc(s_wsp_a, 1)
            for b in range(B):
                act.wait_ge(s_wvf, b + 1)
                nc.scalar.activation(wvo_hi[:, b, :, :], wT_sb[:, b, :, :], ACT.Copy).then_inc(s_wsp_a, 1)
            act.wait_ge(s_mod_mm, 7)
            load_weights(act, MID, EX, s_ld_w2)

            def router_exp(row):
                act.wait_ge(s_rt, row * R_ROW + R_SHIFTED)
                nc.scalar.activation(cw, cw, ACT.Exp).then_inc(s_rexp, 1)

            def cw_evac(row):
                act.wait_ge(s_cwT_mm, row + 1)
                nc.scalar.activation(cwT, ps[0:E, TR:TR + 2, :].rearrange("p b n -> p (b n)"), ACT.Copy
                                     ).then_inc(s_cwT, 1)

            def norm2_hi(t):
                done(act, "h2T", t)
                done(act, "hlo", t - 2)
                for c in range(DC):
                    last = nc.scalar.activation(h2f[:, t % 2, c, :], ps[:, Y0, c * P:(c + 1) * P], ACT.Identity,
                                                scale=mod_cols[:, t // NT, 1, c:c + 1],
                                                bias=mod_cols[:, t // NT, 0, c:c + 1])
                last.then_inc(tl["h2f"], 1)
                done(act, "h2f", t)
                nc.scalar.activation(h2T_hi[:, :, t * P:(t + 1) * P], h2f[:, t % 2, :, :], ACT.Copy
                                     ).then_inc(tl["hhi"], 1)

            for s in range(FIRST, LAST + 1):
                t = s - 1
                if 0 <= t < TILES:
                    for u, first, n in units_of(t):
                        done(act, "pT", u)
                        if u >= PT_RING:
                            done(act, "pv", tile_of_unit(u - PT_RING))
                        nc.scalar.activation(pT_hi[:, u % PT_RING, 0:n * P], ps[:, X0 + u % 2, 0:n * P],
                                             ACT.Copy).then_inc(tl["pthi"], 1)
                t = s + 3
                if 0 <= t < TILES:
                    done(act, "shift2", t)
                    done(act, "xT", t - 2)
                    nc.scalar.activation(xn[:, t % 2, :], h[:, t % 2, :], ACT.Identity,
                                         scale=rstd[:, 1, t % 4:t % 4 + 1], bias=shift[:, 1, t % 4:t % 4 + 1]
                                         ).then_inc(tl["xn"], 1)
                t = s + 2
                if 0 <= t < TILES:
                    at = slot_of(t) * P
                    done(act, "xT", t)
                    if t == 0:
                        act.wait_ge(s_ld_cols, 32)
                    done(act, "xlo", t - 2)
                    for c in range(DC):
                        last = nc.scalar.activation(xf[:, t % 2, c, :], ps[:, Y0, c * P:(c + 1) * P], ACT.Identity,
                                                    scale=cols[:, 0, c:c + 1], bias=cols[:, 1, c:c + 1])
                    last.then_inc(tl["xf"], 1)
                    done(act, "xf", t)
                    if t >= KEY_SLOTS:
                        done(act, "scores", NT - 1)
                    nc.scalar.activation(xnT_hi[:, :, at:at + P], xf[:, t % 2, :, :], ACT.Copy
                                         ).then_inc(tl["xhi"], 1)
                t = s
                if 0 <= t < TILES:
                    done(act, "negmax", t)
                    if t >= 2:
                        done(act, "pT", units_of(t - 2)[-1][0])
                    done(act, "rinv", t - 4)
                    nc.scalar.activation(probs[:, t % 2, 0:(t % NT + 1) * P], score_banks(t), ACT.Exp,
                                         bias=negmax[:, t % 4:t % 4 + 1],
                                         accum_out=rowsum[:, t % 4:t % 4 + 1]).then_inc(tl["exp"], 1)
                t = s + 1
                if 0 <= t < TILES:
                    done(act, "vq", t)
                    done(act, "scores", t - 2)
                    if t >= KEY_SLOTS:
                        done(act, "pv", NT - 1)
                    nc.scalar.activation(vq(V_HI, Q_HI, t), ps[:, Y1, :].rearrange("p (two x) -> p two x", two=2),
                                         ACT.Copy).then_inc(tl["vqhi"], 1)
                if 0 <= s - 2 < TILES:
                    norm2_hi(s - 2)
                if s == ROUTE:
                    act.wait_ge(s_lgT_mm, 1)
                    nc.scalar.activation(logitsT.rearrange("p (b n) -> p b n", n=BANK), ps[0:E, 1:4:2, :], ACT.Copy
                                         ).then_inc(s_lgT, 1)
                if s == ROUTE + 2:
                    router_exp(0)

            def split_hi(e, k, n):
                if not (isinstance(n, int) and n < UN):
                    act.wait_ge(s_y, n - UN + 1)
                src = w_raw[:, e, :] if isinstance(e, int) else w_raw[:, bass.ds(e, 1), :].rearrange("p a w -> p (a w)")
                nc.scalar.activation(w_hi[k], src, ACT.Copy).then_inc(s_whi, 1)

            def silu_step(k, n):
                act.wait_ge(s_ab, n + 1)
                if not (isinstance(n, int) and n < 2):
                    act.wait_ge(s_glo, n - 2 + 1)
                nc.scalar.activation(act_g[:, k % 2, :], ps[:, 2 * (k % 2), :], ACT.Silu).then_inc(s_silu, 1)

            def g_hi_step(k, n):
                act.wait_ge(s_g, n + 1)
                if not (isinstance(n, int) and n < 2):
                    act.wait_ge(s_y, n - 2 + 1)
                nc.scalar.activation(g_hi[:, k % 2, :], act_g[:, k % 2, :], ACT.Copy).then_inc(s_ghi, 1)

            def evac(b):
                act.wait_ge(s_y, b * EX + EX)
                if not (isinstance(b, int) and b == 0):
                    act.wait_ge(s_yT_mm, b)
                nc.scalar.activation(yT[:, 0, :], ps[:, 4, :], ACT.Copy).then_inc(s_ya, 1)

            def group(b, g, static=False, evac_of=None, last=False):
                for k in range(UN):
                    n = b * EX + (g * UN + k)
                    silu_step(k, n)
                    e = g * UN + k + 2
                    if static and e >= EX:
                        if not last:
                            split_hi(e - EX, (k + 2) % UN, n + 2)
                    else:
                        split_hi(e, (k + 2) % UN, n + 2)
                    if k == 1 and evac_of is not None:
                        evac(evac_of)
                    g_hi_step(k, n)

            def rest(b, first=1, last=False):
                with act.Fori(first, NG - 1) as g:
                    group(b, g)
                group(b, NG - 1, static=True, last=last)

            def logits_row1():
                act.wait_ge(s_lgT_mm, 2)
                act.wait_ge(s_cwst, 16)
                nc.scalar.activation(logitsT, ps[0:E, TR:TR + 2, :].rearrange("p b n -> p (b n)"), ACT.Copy
                                     ).then_inc(s_lgT, 1)

            between = {(0, 0): lambda: norm2_hi(TILES - 1), (0, 1): lambda: cw_evac(0),
                       (0, 2): logits_row1, (1, 1): lambda: router_exp(1), (1, 3): lambda: cw_evac(1)}
            act.wait_ge(s_ld_w, 10 * 16)
            split_hi(0, 0, 0)
            split_hi(1, 1, 1)
            for g in range(2):
                for k in range(UN):
                    n = g * UN + k
                    silu_step(k, n)
                    if (g, k) in between:
                        between[g, k]()
                    split_hi(n + 2, (k + 2) % UN, n + 2)
                    g_hi_step(k, n)
            act.wait_ge(s_ld_w2, 5 * 16)
            act.wait_ge(s_ld_w3, 5 * 16)
            rest(0, first=2)
            group(1, 0, static=True, evac_of=0)
            with act.Fori(1, NB - 1) as b:
                rest(b)
                group(b + 1, 0, static=True, evac_of=b)
            rest(NB - 1, last=True)
            evac(NB - 1)

        @block.vector
        def _(dve):
            dve.wait_ge(s_siluc, 1)
            dve.wait_ge(s_const, 1)
            for b in range(B):
                for c in range(DC):
                    nc.vector.memset(silu_b[:, b, c, :], 1.0).then_inc(s_silub, 1)
            dve.wait_ge(s_silub, 4)
            for b in range(B):
                for c in range(DC):
                    nc.vector.tensor_scalar(silu_b[:, b, c, :], silu_b[:, b, c, :], silu_c[:, b, c:c + 1], None,
                                            ALU.mult).then_inc(s_silub, 1)
            for b in range(B):
                dve.wait_ge(s_mod_mm, b + 1)
                nc.vector.tensor_copy(mod[:, b, 0:D], ps[:, b, 0:D])
                last = nc.vector.tensor_scalar(mod[:, b, D:2 * D], ps[:, b, D:2 * D], 1.0, None, ALU.add)
            last.then_inc(s_modev, 1)
            dve.wait_ge(s_wsp_a, 1)
            nc.vector.tensor_tensor(wr_lo[:], wr_raw, wr_hi[:].bitcast(F32), ALU.subtract).then_inc(s_wsp_d, 1)
            dve.wait_ge(s_wt_mm, 2)
            nc.vector.tensor_copy(wT_sb[:, 1, :, :], ps[:, 7, :].rearrange("p (k c) -> p k c", k=DC)
                                  ).then_inc(s_wt_d, 1)

            gates = [0]

            def gate(dst, src):
                def then(ins):
                    gates[0] += 1
                    ins.then_inc(s_gt, 1)

                then(nc.vector.tensor_scalar(gate_tmp, src, 0.0, 2.0, ALU.is_ge, ALU.mult))
                then(nc.vector.tensor_copy(dst, src))
                dve.wait_ge(s_gt, gates[0])
                then(nc.vector.scalar_tensor_tensor(out=dst, in0=dst, scalar=-1.0, in1=dst, op0=ALU.mult, op1=ALU.max))
                dve.wait_ge(s_gt, gates[0])
                then(nc.vector.tensor_scalar(dst, dst, GATE_FLOOR, None, ALU.max))
                dve.wait_ge(s_gt, gates[0])
                then(nc.vector.scalar_tensor_tensor(out=dst, in0=gate_tmp, scalar=-1.0, in1=dst, op0=ALU.add,
                                                    op1=ALU.mult))
                dve.wait_ge(s_gt, gates[0])

            for b in range(B):
                dve.wait_ge(s_mod_mm, 3 + b)
                gate(mod[:, b, 2 * D:3 * D], ps[:, 2 + b, 0:D])
            nc.vector.tensor_copy(gate_tmp[:, 0:1], gate_tmp[:, 0:1]).then_inc(s_modev, 2)
            dve.wait_ge(s_wqk_mm, 1)
            dve.wait_ge(s_wsp_a, 2)
            nc.vector.scalar_tensor_tensor(out=wqk_lo, in0=ps[:, 6, :].rearrange("p (c d) -> p c d", c=DC),
                                           scalar=D ** -0.5, in1=wqk_hi.bitcast(F32), op0=ALU.mult,
                                           op1=ALU.subtract).then_inc(s_wsp_d, 1)
            dve.wait_ge(s_wvo_mm, 1)
            dve.wait_ge(s_modev, 3)
            for b in range(B):
                for c in range(DC):
                    last = nc.vector.tensor_tensor(wT_sb[:, b, c, :], ps[:, 7, c * D:(c + 1) * D],
                                                   mod[:, b, 2 * D:3 * D], ALU.mult)
                last.then_inc(s_wvf, 1)
            for b in range(B):
                dve.wait_ge(s_wsp_a, 3 + b)
                dve.wait_ge(s_wvf, b + 1)
                nc.vector.tensor_tensor(wvo_lo[:, b, :, :], wT_sb[:, b, :, :], wvo_hi[:, b, :, :].bitcast(F32),
                                        ALU.subtract).then_inc(s_wsp_d, 1)
            dve.wait_ge(s_mod_mm, 5)
            for half in range(2):
                for c in range(DC):
                    src = ps[:, 5, (half * DC + c) * B:(half * DC + c + 1) * B]
                    last = nc.vector.tensor_scalar(mod_cols[:, :, half, c], src, float(half), None, ALU.add)
            last.then_inc(s_modev, 1)
            for b in range(B):
                dve.wait_ge(s_mod_mm, 7)
                gate(gate_b[:, 2 * b, :], ps[:, 4, b * D:(b + 1) * D])
                nc.vector.tensor_copy(gate_b[:, 2 * b + 1, :], gate_b[:, 2 * b, :]).then_inc(s_modev, 1)

            def stats(n, src, t):
                done(dve, f"stat{n}", t - 4)
                nc.vector.bn_stats(bn[:, n - 1, t % 4, :], src).then_inc(tl[f"bn{n}"], 1)

            def stats_end(n, t, *read_by):
                done(dve, f"bn{n}", t)
                for stage_ in read_by:
                    done(dve, stage_, t - 4)
                nc.vector.bn_aggr(mv[:, n - 1, t % 4, :], bn[:, n - 1, t % 4, :]).then_inc(tl[f"stat{n}"], 1)

            def norm2_lo(t):
                done(dve, "hhi", t)
                nc.vector.tensor_tensor(h2T_lo[:, :, t * P:(t + 1) * P], h2f[:, t % 2, :, :],
                                        h2T_hi[:, :, t * P:(t + 1) * P].bitcast(F32), ALU.subtract
                                        ).then_inc(tl["hlo"], 1)

            chain = [0]

            def link(ins):
                chain[0] += 1
                ins.then_inc(s_rt, 1)

            def settle():
                dve.wait_ge(s_rt, chain[0])

            full = (P, NT, E)

            def route_top(row):
                lg = logits[:, row * NT:(row + 1) * NT, :]
                dve.wait_ge(s_lg_mm, row + 1)
                nc.vector.tensor_copy(lg, ps[:, Y0, 0:NT * E].rearrange("p (t e) -> p t e", e=E)).then_inc(s_lg, 1)
                dve.wait_ge(s_lg, row + 1)
                for t in range(NT):
                    link(nc.vector.max(top8[:, t, :], lg[:, t, :]))
                settle()
                dve.wait_ge(s_cwT_mm, row)
                link(nc.vector.tensor_tensor(cw, lg, top8[:, :, 0:1].broadcast_to(full), ALU.subtract))
                assert chain[0] == row * R_ROW + R_SHIFTED

            def route_select(row):
                lg = logits[:, row * NT:(row + 1) * NT, :]
                fourth = top8[:, :, TOPK - 1:TOPK].broadcast_to(full)
                link(nc.vector.tensor_tensor(above, lg, fourth, ALU.is_gt))
                link(nc.vector.tensor_tensor(ties, lg, fourth, ALU.is_equal))
                link(nc.vector.memset(reset, 1.0))
                settle()
                link(nc.vector.memset(reset[:, :, 0:1], 0.0))
                link(nc.vector.tensor_reduce(need, above, AX.X, ALU.add))
                settle()
                link(nc.vector.tensor_scalar(need, need, -1.0, float(TOPK), ALU.mult, ALU.add))
                link(nc.vector.tensor_tensor_scan(nth_tie.rearrange("p t e -> p (t e)"),
                                                  reset.rearrange("p t e -> p (t e)"),
                                                  ties.rearrange("p t e -> p (t e)"), 0.0, ALU.mult, ALU.add))
                settle()
                link(nc.vector.tensor_tensor(nth_tie, nth_tie, need.broadcast_to(full), ALU.is_le))
                settle()
                link(nc.vector.tensor_tensor(ties, ties, nth_tie, ALU.mult))
                settle()
                link(nc.vector.tensor_tensor(ties, ties, above, ALU.add))

            def route_weights(row):
                settle()
                dve.wait_ge(s_rexp, row + 1)
                link(nc.vector.tensor_tensor(cw, cw, ties, ALU.mult))
                settle()
                link(nc.vector.tensor_reduce(total, cw, AX.X, ALU.add))
                settle()
                link(nc.vector.reciprocal(total, total))
                settle()
                link(nc.vector.tensor_scalar(total, total, TOPK / (TOPK + 1.0), None, ALU.mult))
                settle()
                link(nc.vector.tensor_tensor(cw, cw, total.broadcast_to(full), ALU.mult))
                assert chain[0] == (row + 1) * R_ROW

            for s in range(FIRST, LAST + 1):
                t = s - 1
                if 0 <= t < TILES:
                    for u, first, n in units_of(t):
                        done(dve, "pthi", u)
                        nc.vector.tensor_tensor(pT_lo[:, u % PT_RING, 0:n * P], ps[:, X0 + u % 2, 0:n * P],
                                                pT_hi[:, u % PT_RING, 0:n * P].bitcast(F32), ALU.subtract
                                                ).then_inc(tl["ptlo"], 1)
                t = s
                if 0 <= t < TILES:
                    done(dve, "scores", t)
                    done(dve, "exp", t - 4)
                    nc.vector.tensor_reduce(negmax[:, t % 4:t % 4 + 1], score_banks(t), AX.X, ALU.max,
                                            negate=True).then_inc(tl["negmax"], 1)
                a, c = s + 5, s + 4
                if a < TILES:
                    dve.wait_ge(s_x[a % 4], (a // 4 + 1) * 16)
                    stats(1, x_in[:, a % 4, :], a)
                if 0 <= c < TILES:
                    done(dve, "stat1", c)
                    done(dve, "resid", c - 2)
                    done(dve, "xn", c - 2)
                    if c == 0:
                        dve.wait_ge(s_modev, 1)
                    nc.vector.scalar_tensor_tensor(out=h[:, c % 2, :], in0=x_in[:, c % 4, :],
                                                   scalar=mv[:, 0, c % 4, 0:1], in1=mod[:, c // NT, D:2 * D],
                                                   op0=ALU.subtract, op1=ALU.mult).then_inc(tl["u"], 1)
                if a < TILES:
                    stats_end(1, a, "u", "eps1")
                t = s + 2
                if 0 <= t < TILES:
                    at = slot_of(t) * P
                    done(dve, "xhi", t)
                    nc.vector.tensor_tensor(xnT_lo[:, :, at:at + P], xf[:, t % 2, :, :],
                                            xnT_hi[:, :, at:at + P].bitcast(F32), ALU.subtract
                                            ).then_inc(tl["xlo"], 1)
                if 0 <= c < TILES:
                    done(dve, "rstd1", c)
                    done(dve, "u", c)
                    nc.vector.scalar_tensor_tensor(out=h[:, c % 2, :], in0=h[:, c % 2, :],
                                                   scalar=rstd[:, 0, c % 4:c % 4 + 1], in1=mod[:, c // NT, 0:D],
                                                   op0=ALU.mult, op1=ALU.add).then_inc(tl["h"], 1)
                t = s + 1
                if 0 <= t < TILES:
                    done(dve, "vqhi", t)
                    nc.vector.tensor_tensor(vq(V_LO, Q_LO, t), ps[:, Y1, :].rearrange("p (two x) -> p two x", two=2),
                                            vq(V_HI, Q_HI, t).bitcast(F32), ALU.subtract).then_inc(tl["vqlo"], 1)
                if 0 <= c < TILES:
                    done(dve, "h", c)
                    stats(2, h[:, c % 2, :], c)
                t = s - 1
                if 0 <= t < TILES:
                    done(dve, "exp", t)
                    done(dve, "x1", t - 4)
                    nc.vector.reciprocal(rinv[:, t % 4:t % 4 + 1], rowsum[:, t % 4:t % 4 + 1]
                                         ).then_inc(tl["rinv"], 1)
                if 0 <= c < TILES:
                    stats_end(2, c, "shift2")
                if 0 <= s - 2 < TILES:
                    norm2_lo(s - 2)
                t = s - 1
                if 0 <= t < TILES:
                    done(dve, "rinv", t)
                    done(dve, "resid", t)
                    done(dve, "pv", t)
                    nc.vector.scalar_tensor_tensor(out=x1[:, t, :], in0=ps[:, Y1, 0:D],
                                                   scalar=rinv[:, t % 4:t % 4 + 1], in1=x1[:, t, :],
                                                   op0=ALU.mult, op1=ALU.add).then_inc(tl["x1"], 1)
                    done(dve, "x1", t)
                    stats(3, x1[:, t, :], t)
                    stats_end(3, t, "shift3")
                if s == ROUTE + 1:
                    route_top(0)
                if s == ROUTE + 2:
                    route_select(0)
                if s == ROUTE + 3:
                    route_weights(0)

            def step(k, n, slot_round, between=None):
                dve.wait_ge(s_silu, n + 1)
                nc.vector.tensor_tensor(act_g[:, k % 2, :], act_g[:, k % 2, :], ps[:, 2 * (k % 2) + 1, :],
                                        ALU.mult).then_inc(s_up, 1)
                dve.wait_ge(s_up, n + 1)
                dve.wait_ge(s_cwb[k % 2], slot_round * 16)
                nc.vector.tensor_tensor(act_g[:, k % 2, :], act_g[:, k % 2, :], cwb[:, k % 2, :], ALU.mult
                                        ).then_inc(s_g, 1)
                if between is not None:
                    between()
                dve.wait_ge(s_ghi, n + 1)
                if not (isinstance(n, int) and n < 2):
                    dve.wait_ge(s_y, n - 2 + 1)
                nc.vector.tensor_tensor(g_lo[:, k % 2, :], act_g[:, k % 2, :], g_hi[:, k % 2, :].bitcast(F32),
                                        ALU.subtract).then_inc(s_glo, 1)

            def evac(b):
                dve.wait_ge(s_y, b * EX + EX)
                if not (isinstance(b, int) and b == 0):
                    dve.wait_ge(s_yT_mm, b)
                nc.vector.tensor_copy(yT[:, 1, :], ps[:, 5, :]).then_inc(s_yd, 1)

            def gated(b):
                dve.wait_ge(s_yT_mm, b + 1)
                if not (isinstance(b, int) and b == 0):
                    dve.wait_ge(s_out, b * 16)
                g_b = gate_b[:, b:b + 1, :] if isinstance(b, int) else gate_b[:, bass.ds(b, 1), :]
                nc.vector.tensor_tensor(y_out, ps[:, TR:TR + 2, :].rearrange("p k (t d) -> p (k t) d", d=D),
                                        g_b.broadcast_to((P, BT, D)), ALU.mult).then_inc(s_gated, 1)

            def group(b, g, evac_of=None):
                for k in range(UN):
                    between = (lambda: evac(evac_of)) if k == 1 and evac_of is not None else None
                    step(k, b * EX + (g * UN + k), b * (EX // 2) + (g * 2 + (k // 2 + 1)), between)

            def rest(b, first=1):
                with dve.Fori(first, NG) as g:
                    group(b, g)

            between = {(0, 0): lambda: norm2_lo(TILES - 1)}
            after = {(0, 3): lambda: route_top(1), (1, 0): lambda: route_select(1), (1, 1): lambda: route_weights(1)}
            for g in range(2):
                for k in range(UN):
                    step(k, g * UN + k, g * 2 + k // 2 + 1, between.get((g, k)))
                    if (g, k) in after:
                        after[g, k]()
            rest(0, first=2)
            group(1, 0, evac_of=0)
            gated(0)
            with dve.Fori(1, NB - 1) as b:
                rest(b)
                group(b + 1, 0, evac_of=b)
                gated(b)
            rest(NB - 1)
            evac(NB - 1)
            gated(NB - 1)

        @block.tensor
        def _(pe):
            def split3(dst, w, x_, first, last):
                nc.tensor.matmul(dst, w[0], x_[0], start=first, stop=False)
                nc.tensor.matmul(dst, w[0], x_[1], start=False, stop=False)
                return nc.tensor.matmul(dst, w[1], x_[0], start=False, stop=last)

            def modulation(dst, n0, n1, b):
                for c in range(DC):
                    last = nc.tensor.matmul(dst, silu_b[:, b, c, :], wmod_sb[:, c, n0:n1], start=(c == 0),
                                            stop=(c == DC - 1))
                last.then_inc(s_mod_mm, 1)

            pe.wait_ge(s_silub, 8)
            pe.wait_ge(s_ld_wmod[0], 16)
            for b in range(B):
                modulation(ps[:, b, :], 0, 2 * D, b)
            pe.wait_ge(s_const, 7)
            pe.wait_ge(s_ld_qkv, 16)
            for m, bank in ((0, 6), (1, 7), (2, 5)):
                for k in range(DC):
                    for c in range(DC):
                        last = nc.tensor.transpose(ps[:, bank, k * D + c * P:k * D + (c + 1) * P],
                                                   qkv_sb[:, c, m * D + k * P:m * D + (k + 1) * P], ident[:])
                last.then_inc(s_wt_mm, 1)
            pe.wait_ge(s_ld_wmod[1], 16)
            for b in range(B):
                modulation(ps[:, 2 + b, 0:D], 2 * D, 3 * D, b)
            pe.wait_ge(s_wt_a, 1)
            pe.wait_ge(s_wt_d, 1)
            for c in range(DC):
                for k in range(DC):
                    last = nc.tensor.matmul(ps[:, 6, c * D:(c + 1) * D], wT_sb[:, 0, k, c * P:(c + 1) * P],
                                            wT_sb[:, 1, k, :], start=(k == 0), stop=(k == DC - 1))
            last.then_inc(s_wqk_mm, 1)
            pe.wait_ge(s_wt_a, 2)
            pe.wait_ge(s_ld_o, 16)
            for c in range(DC):
                for k in range(DC):
                    last = nc.tensor.matmul(ps[:, 7, c * D:(c + 1) * D], wT_sb[:, 2, k, c * P:(c + 1) * P],
                                            o_sb[:, k, :], start=(k == 0), stop=(k == DC - 1))
            last.then_inc(s_wvo_mm, 1)
            pe.wait_ge(s_ld_wmod[2], 16)
            pe.wait_ge(s_wt_a, 2)
            for half in range(2):
                for m in range(DC):
                    n0 = (3 + half) * D + m * P
                    for c in range(DC):
                        last = nc.tensor.matmul(ps[:, 5, (half * DC + m) * B:(half * DC + m + 1) * B],
                                                wmod_sb[:, c, n0:n0 + P], silu_c[:, :, c],
                                                start=(c == 0), stop=(c == DC - 1))
            last.then_inc(s_mod_mm, 1)
            for b in range(B):
                modulation(ps[:, 4, b * D:(b + 1) * D], 5 * D, 6 * D, b)

            def transpose_back(t):
                done(pe, "z2", t)
                done(pe, "xf", min(t + 4, TILES - 1))
                done(pe, "h2f", t - 1)
                if t == TILES - 1:
                    done(pe, "h2f", t - 1)
                for c in range(DC):
                    last = nc.tensor.transpose(ps[:, Y0, c * P:(c + 1) * P], z2[:, t % 2, c * P:(c + 1) * P],
                                               ident[:])
                last.then_inc(tl["h2T"], 1)

            def logits_product(row, banks):
                done(pe, "hlo", (row + 1) * NT - 1)
                for half in range(S // TB):
                    tok = slice(row * S + half * TB, row * S + (half + 1) * TB)
                    for c in range(DC):
                        last = split3(ps[:, banks[half], :], (wr_hi[:, c, :], wr_lo[:, c, :]),
                                      (h2T_hi[:, c, tok], h2T_lo[:, c, tok]), c == 0, c == DC - 1)
                last.then_inc(s_lgT_mm, 1)

            def logits_back(row):
                pe.wait_ge(s_lgT, row + 1)
                for t in range(NT):
                    last = nc.tensor.transpose(ps[:, Y0, t * E:(t + 1) * E], logitsT[:, t * P:(t + 1) * P],
                                               ident[0:E, 0:E])
                last.then_inc(s_lg_mm, 1)

            def cw_rows(row):
                pe.wait_ge(s_rt, (row + 1) * R_ROW)
                for t in range(NT):
                    last = nc.tensor.transpose(ps[0:E, TR + t // BT, (t % BT) * P:(t % BT + 1) * P], cw[:, t, :],
                                               ident[:])
                last.then_inc(s_cwT_mm, 1)

            pe.wait_ge(s_constr, 2)
            pe.wait_ge(s_wsp_d, 4)
            for s in range(FIRST, LAST + 1):
                t = s - 1
                if 0 <= t < TILES:
                    if t == 0:
                        pe.wait_ge(s_modev, 6)
                    done(pe, "exp", t)
                    for u, first, n in units_of(t):
                        done(pe, "ptlo", u - 2)
                        for j in range(n):
                            last = nc.tensor.transpose(ps[:, X0 + u % 2, j * P:(j + 1) * P],
                                                       probs[:, t % 2, (first + j) * P:(first + j + 1) * P], ident[:])
                        last.then_inc(tl["pT"], 1)
                t = s
                if 0 <= t < TILES:
                    done(pe, "vqlo", t)
                    done(pe, "exp", t - 2)
                    if t == NT + BT:
                        pe.wait_ge(s_lgT, 1)
                    row0, i = t // NT * NT, t % NT
                    for first in range(0, i + 1, BT):
                        end = min(first + BT, i + 1)
                        dst = ps[:, 2 * (t % 2) + first // BT, :]
                        own = end == i + 1
                        for off, slot, n in key_runs(row0 + first, row0 + end):
                            masked = own and first + off + n == end
                            keys = slice(slot * P, (slot + n) * P)
                            for c in range(DC):
                                last = split3(dst[:, off * P:(off + n) * P], (qT_hi[:, t % 2, c, :], qT_lo[:, t % 2, c, :]),
                                              (xnT_hi[:, c, keys], xnT_lo[:, c, keys]), c == 0,
                                              c == DC - 1 and not masked)
                        if own:
                            last = nc.tensor.matmul(dst[:, (i - first) * P:(i - first + 1) * P], ident_r[:], mask_r[:],
                                                    start=False, stop=True)
                    last.then_inc(tl["scores"], 1)
                t = s + 2
                if 0 <= t < TILES:
                    done(pe, "xn", t)
                    done(pe, "xf", t - 1)
                    done(pe, "h2f", t - 5)
                    if t == 0:
                        pe.wait_ge(s_wsp_a, 2)
                    if s == ROUTE + 2:
                        pe.wait_ge(s_lg, 1)
                    for c in range(DC):
                        last = nc.tensor.transpose(ps[:, Y0, c * P:(c + 1) * P], xn[:, t % 2, c * P:(c + 1) * P],
                                                   ident[:])
                    last.then_inc(tl["xT"], 1)
                t = s + 1
                if 0 <= t < TILES:
                    done(pe, "xlo", t)
                    done(pe, "x1", t - 3)
                    done(pe, "vqlo", t - 1)
                    tok = slice(slot_of(t) * P, (slot_of(t) + 1) * P)
                    for c in range(DC):
                        split3(ps[:, Y1, 0:D], (xnT_hi[:, c, tok], xnT_lo[:, c, tok]),
                               (wvo_hi[:, t // NT, c, :], wvo_lo[:, t // NT, c, :]), c == 0, c == DC - 1)
                    for m in range(DC):
                        for c in range(DC):
                            last = split3(ps[:, Y1, D + m * P:D + (m + 1) * P],
                                          (wqk_hi[:, c, m * P:(m + 1) * P], wqk_lo[:, c, m * P:(m + 1) * P]),
                                          (xnT_hi[:, c, tok], xnT_lo[:, c, tok]), c == 0, c == DC - 1)
                    last.then_inc(tl["vq"], 1)
                if 0 <= s - 2 < TILES:
                    transpose_back(s - 2)
                t = s - 1
                if 0 <= t < TILES:
                    done(pe, "vqlo", min(t + 2, TILES - 1))
                    done(pe, "x1", t - 1)
                    row0, i = t // NT * NT, t % NT
                    for u, first, n in units_of(t):
                        done(pe, "ptlo", u)
                        for j in range(n):
                            slot = slot_of(row0 + first + j)
                            last = split3(ps[:, Y1, 0:D],
                                          [m[:, u % PT_RING, j * P:(j + 1) * P] for m in (pT_hi, pT_lo)],
                                          [m[:, slot, :] for m in (v_hi, v_lo)],
                                          first + j == 0, first + j == i)
                    last.then_inc(tl["pv"], 1)
                if s == ROUTE:
                    done(pe, "exp", NT - 1)
                    logits_product(0, (1, 3))
                if s == ROUTE + 1:
                    done(pe, "h2f", s - 2)
                    logits_back(0)

            def gate_up(b, k, n):
                pe.wait_ge(s_wlo, n + 1)
                if not (isinstance(n, int) and n < 2):
                    pe.wait_ge(s_up, n - 2 + 1)
                tok = slice(b * TB, (b + 1) * TB) if isinstance(b, int) else bass.ds(b * TB, TB)
                for bank, at_ in ((2 * (k % 2), W1), (2 * (k % 2) + 1, W3)):
                    for c in range(DC):
                        cols_ = slice(at_ + c * P, at_ + (c + 1) * P)
                        last = split3(ps[:, bank, :], (w_hi[k][:, cols_], w_lo[k][:, cols_]),
                                      (h2T_hi[:, c, tok], h2T_lo[:, c, tok]), c == 0, c == DC - 1)
                last.then_inc(s_ab, 1)

            def down(k, n, first=False, final=False, drained=None):
                pe.wait_ge(s_glo, n + 1)
                if drained is not None:
                    pe.wait_ge(s_ya, drained)
                    pe.wait_ge(s_yd, drained)
                for c in range(DC):
                    cols_ = slice(W2 + c * P, W2 + (c + 1) * P)
                    last = split3(ps[:, 4 + c, :], (w_hi[k][:, cols_], w_lo[k][:, cols_]),
                                  (g_hi[:, k % 2, :], g_lo[:, k % 2, :]), first, final)
                last.then_inc(s_y, 1)

            def turn_back(b):
                pe.wait_ge(s_ya, b + 1)
                pe.wait_ge(s_yd, b + 1)
                if not (isinstance(b, int) and b == 0):
                    pe.wait_ge(s_gated, b)
                for j in range(BT):
                    for c in range(DC):
                        last = nc.tensor.transpose(
                            ps[:, TR + j // 2, (j % 2) * D + c * P:(j % 2) * D + (c + 1) * P],
                            yT[:, c, j * P:(j + 1) * P], ident[:])
                last.then_inc(s_yT_mm, 1)

            def head(b, before):
                for k in range(UN):
                    n = b * EX + k
                    gate_up(b, k, n)
                    if k >= 2:
                        down(k - 2, n - 2, first=(k == 2), drained=before + 1)
                    else:
                        down(k + 2, n - 2, final=(k == 1))
                turn_back(before)

            def rest(b, first=1):
                with pe.Fori(first, NG) as g:
                    for k in range(UN):
                        n = b * EX + (g * UN + k)
                        gate_up(b, k, n)
                        down((k + 2) % UN, n - 2)

            done(pe, "exp", TILES - 1)

            def logits_row1():
                pe.wait_ge(s_cwT, 1)
                logits_product(1, (TR, TR + 1))

            def cw_row0():
                done(pe, "h2f", TILES - 1)
                done(pe, "x1", TILES - 1)
                cw_rows(0)

            def cw_row1():
                pe.wait_ge(s_lg, 2)
                cw_rows(1)

            after_gate_up = {(0, 0): lambda: transpose_back(TILES - 1), (0, 1): cw_row0, (0, 2): logits_row1,
                             (0, 3): lambda: logits_back(1), (1, 3): cw_row1}
            for g in range(2):
                for k in range(UN):
                    n = g * UN + k
                    gate_up(0, k, n)
                    if (g, k) in after_gate_up:
                        after_gate_up[g, k]()
                    if n >= 2:
                        down((k + 2) % UN, n - 2, first=(n == 2))
            rest(0, first=2)
            pe.wait_ge(s_cwT, 2)
            head(1, before=0)
            with pe.Fori(1, NB - 1) as b:
                rest(b)
                head(b + 1, before=b)
            rest(NB - 1)
            down(2, NB * EX - 2)
            down(3, NB * EX - 1, final=True)
            turn_back(NB - 1)


_INS = ['L0_attn_x', 'L0_attn_qkv', 'L0_attn_o_proj', 'L0_attn_gamma', 'L0_attn_beta', 'L0_ffn_w_router',
        'L0_ffn_we1', 'L0_ffn_we3', 'L0_ffn_we2', 'L0_ffn_ws1', 'L0_ffn_ws3', 'L0_ffn_ws2', 'L0_c', 'L0_wmod']
_OUTS = [((B, S, D), 'float32')]


def kernel(**inputs):
    import numpy as _np
    import concourse.bacc as _bacc
    from concourse import mybir as _mybir
    from concourse.bass_utils import run_bass_kernel_spmd as _run

    nc = _bacc.Bacc("TRN2", target_bir_lowering=False, num_devices=1)
    arrays, args = {}, []
    for name in _INS:
        a = _np.ascontiguousarray(inputs[name])
        arrays[f"in_{name}_dram"] = a
        args.append(nc.dram_tensor(f"in_{name}_dram", a.shape, _mybir.dt.from_np(a.dtype), kind="ExternalInput").ap())
    for i, (shape, dtype) in enumerate(_OUTS):
        dt = _mybir.dt.from_np(_np.dtype(dtype))
        args.append(nc.dram_tensor(f"out_{i}_dram", shape, dt, kind="ExternalOutput").ap())
    adaln_block(nc, *args)
    r = _run(nc, [arrays], core_ids=[0])
    return r.results[0]["out_0_dram"]
```

```python
from contextlib import ExitStack

import concourse.bass as bass
from concourse import mybir

F32 = mybir.dt.float32
F32R = mybir.dt.float32r
ALU = mybir.AluOpType
ACT = mybir.ActivationFunctionType
AX = mybir.AxisListType

P = 128
D = 256
DC = D // P
B, S = 2, 1024
T = B * S
NT = S // P
TILES = B * NT
E = 16
TOPK = 4
H = 128
HS = 512
SH = HS // H
EX = SH + E
TB = 512
NB = T // TB
BT = TB // P
EPS = 1e-5
BANK = 512
MASKED = -1e30
GATE_FLOOR = 0.25

W1, W3, W2, WX = 0, D, 2 * D, 3 * D
UN = 4
NG = EX // UN
PEELED = 3
FIRST = -5
LAST = TILES
KEY_SLOTS = NT + 2
EARLY, MID = 11, 16


def slot_of(t):
    return t if t < KEY_SLOTS else t - KEY_SLOTS


def key_runs(first, end):
    runs = []
    for t in range(first, end):
        if runs and slot_of(t) == runs[-1][1] + runs[-1][2]:
            runs[-1][2] += 1
        else:
            runs.append([t - first, slot_of(t), 1])
    return runs


def units_of(t):
    row, i = divmod(t, NT)
    first = row * UNITS + (i if i < BT else BT + 2 * (i - BT))
    return [(first + n // BT, n, min(BT, i + 1 - n)) for n in range(0, i + 1, BT)]


UNITS = BT + 2 * (NT - BT)
PT_RING = 3
ROUTE = NT + 3


def tile_of_unit(u):
    row, v = divmod(u, UNITS)
    return row * NT + (v if v < BT else BT + (v - BT) // 2)


R_SHIFTED = NT + 1
R_ROW = R_SHIFTED + 15


def adaln_block(nc, x, qkv, o_proj, gamma, beta, w_router, we1, we3, we2, ws1, ws3, ws2, c_in, wmod, out):
    cw_dram = nc.dram_tensor("cw_rows", (EX, T), F32, kind="Internal").ap()
    ctx = ExitStack()
    with ctx:
        def sb(name, shape, dt=F32):
            return ctx.enter_context(nc.sbuf_tensor(name, shape, dt))

        def sem(name):
            return ctx.enter_context(nc.semaphore(name))

        w_raw = sb("w_raw", [P, EX, WX])
        h2T_hi = sb("h2T_hi", [P, DC, T], F32R)
        h2T_lo = sb("h2T_lo", [P, DC, T], F32R)
        x1 = sb("x1", [P, B * NT, D])
        mod = sb("mod", [P, B, 3 * D])
        mod_cols = sb("mod_cols", [P, B, 2, DC])
        gate_b = sb("gate_b", [P, NB, D])
        ident = sb("ident", [P, P])
        ident_r = sb("ident_r", [P, P], F32R)
        mask_r = sb("mask_r", [P, P], F32R)
        wr_hi = sb("wr_hi", [P, DC, P], F32R)
        wr_lo = sb("wr_lo", [P, DC, P], F32R)
        logits = sb("logits", [P, TILES, E])
        cols = sb("cols", [P, 4, DC])
        silu_c = sb("silu_c", [P, B, DC])
        minus_half = sb("minus_half", [P, 1])
        eps = sb("eps", [P, 1])
        table_out = sb("table_out", [P, 1])
        bn = sb("bn", [P, 3, 4, 6])
        mv = sb("mv", [P, 3, 4, 2])
        veps = sb("veps", [P, 3, 4])
        rstd = sb("rstd", [P, 3, 4])
        shift = sb("shift", [P, 3, 4])
        negmax = sb("negmax", [P, 4])
        rowsum = sb("rowsum", [P, 4])
        rinv = sb("rinv", [P, 4])

        def w_raw_of(e):
            return w_raw[:, e, :] if isinstance(e, int) else w_raw[:, bass.ds(e, 1), :].rearrange("p a w -> p (a w)")

        rpool = sb("rpool", [P, 17408], F32R)

        def r_part(at, n):
            return rpool[:, at:at + n]

        KS = KEY_SLOTS * P
        V_HI, Q_HI, V_LO, Q_LO = 0, KEY_SLOTS * D, KEY_SLOTS * D + 2 * D, 2 * KEY_SLOTS * D + 2 * D
        v_hi = r_part(V_HI, KEY_SLOTS * D).rearrange("p (t d) -> p t d", d=D)
        v_lo = r_part(V_LO, KEY_SLOTS * D).rearrange("p (t d) -> p t d", d=D)
        qT_hi = r_part(Q_HI, 2 * D).rearrange("p (s c t) -> p s c t", s=2, c=DC)
        qT_lo = r_part(Q_LO, 2 * D).rearrange("p (s c t) -> p s c t", s=2, c=DC)
        xnT_hi = r_part(6144, DC * KS).rearrange("p (c t) -> p c t", c=DC)
        xnT_lo = r_part(8704, DC * KS).rearrange("p (c t) -> p c t", c=DC)
        pT_hi = r_part(11264, 1536).rearrange("p (u k) -> p u k", k=BANK)
        pT_lo = r_part(12800, 1536).rearrange("p (u k) -> p u k", k=BANK)
        wqk_hi = r_part(14336, 512).rearrange("p (c d) -> p c d", c=DC)
        wqk_lo = r_part(14848, 512).rearrange("p (c d) -> p c d", c=DC)
        wvo_hi = r_part(15360, 1024).rearrange("p (b c d) -> p b c d", b=B, c=DC)
        wvo_lo = r_part(16384, 1024).rearrange("p (b c d) -> p b c d", b=B, c=DC)

        def vq(v0, q0, t):
            at = v0 + slot_of(t) * D
            apart = q0 + t % 2 * D - at
            return r_part(at, 2 * apart).rearrange("p (two x) -> p two x", two=2)[:, :, 0:D]

        slots = [14336, 14336 + 2 * WX, 6144, 6144 + 2 * WX]
        w_hi = [r_part(at, WX) for at in slots]
        w_lo = [r_part(at + WX, WX) for at in slots]
        G_HI, G_LO = V_HI + (NT - 2) * D, V_LO + (NT - 2) * D
        g_hi, g_lo = (r_part(at, 4 * TB).rearrange("p (s t) -> p s t", s=2)[:, :, 0:TB] for at in (G_HI, G_LO))
        assert G_HI + 2 * TB == Q_HI and G_LO + 2 * TB == Q_LO

        fpool = sb("fpool", [P, 4096])

        def f_part(at, n):
            return fpool[:, at:at + n]

        x_in = f_part(0, 1024).rearrange("p (s d) -> p s d", s=4)
        h = f_part(1024, 512).rearrange("p (s d) -> p s d", s=2)
        xn = f_part(1536, 512).rearrange("p (s d) -> p s d", s=2)
        logitsT = fpool[0:E, 2048:2048 + S]
        cwT = logitsT
        xf = f_part(3072, 512).rearrange("p (s c t) -> p s c t", s=2, c=DC)
        z2 = f_part(3584, 512).rearrange("p (s d) -> p s d", s=2)
        act_g = f_part(0, 2 * TB).rearrange("p (s t) -> p s t", s=2)
        cwb = f_part(1024, 2 * TB).rearrange("p (s t) -> p s t", s=2)
        yT = f_part(2048, DC * TB).rearrange("p (c t) -> p c t", c=DC)
        y_out = f_part(3072, BT * D).rearrange("p (t d) -> p t d", t=BT)
        gate_tmp = f_part(2304, D)
        silu_b = f_part(3584, 512).rearrange("p (b c q) -> p b c q", b=B, c=DC)
        wr_raw = f_part(2048, DC * P).rearrange("p (c e) -> p c e", c=DC)
        mask_raw = f_part(3072, P)
        shared_row = sb("shared_row", [SH, P])
        stage = w_raw[:, EARLY:EX, :].rearrange("p e w -> p (e w)")
        qkv_sb = stage[:, 0:1536].rearrange("p (c n) -> p c n", c=DC)
        o_sb = stage[:, 1536:2048].rearrange("p (c n) -> p c n", c=DC)
        wT_sb = stage[:, 2048:3584].rearrange("p (m k c) -> p m k c", m=3, k=DC)
        wmod_sb = stage[:, 3584:6656].rearrange("p (c n) -> p c n", c=DC)
        probs = stage[:, 0:2048].rearrange("p (s k) -> p s k", s=2)
        h2f = stage[:, 2048:2560].rearrange("p (s c t) -> p s c t", s=2, c=DC)
        rt = mod[:, 0, :]
        top8 = rt[:, 0:64].rearrange("p (t k) -> p t k", k=8)
        above = rt[:, 64:192].rearrange("p (t e) -> p t e", e=E)
        ties = rt[:, 192:320].rearrange("p (t e) -> p t e", e=E)
        nth_tie = rt[:, 320:448].rearrange("p (t e) -> p t e", e=E)
        cw = rt[:, 448:576].rearrange("p (t e) -> p t e", e=E)
        reset = rt[:, 576:704].rearrange("p (t e) -> p t e", e=E)
        need = rt[:, 704:712].rearrange("p (t e) -> p t e", e=1)
        total = rt[:, 712:720].rearrange("p (t e) -> p t e", e=1)

        ps = ctx.enter_context(nc.psum_tensor("ps", [P, 8, BANK], F32))
        X0, Y0, Y1, TR = 4, 6, 7, 6

        def score_banks(t):
            return ps[:, 2 * (t % 2):2 * (t % 2) + 2, :].rearrange("p b n -> p (b n)")[:, 0:(t % NT + 1) * P]

        def pv_out(t):
            if t == TILES - 1:
                return ps[:, Y1, 0:D]
            if NT <= t < NT + 2:
                return ps[:, 2 * (t % 2), BANK - D:BANK]
            return ps[:, 2 * (t % 2) + 1, 0:D]

        s_ld_c, s_ld_cols, s_ld_qkv, s_ld_o, s_ld_wr = (sem(n) for n in (
            "ld_c", "ld_cols", "ld_qkv", "ld_o", "ld_wr"))
        s_ld_wmod = [sem(f"ld_wmod{n}") for n in range(3)]
        s_ld_w = sem("ld_w_early")
        s_ld_w2 = sem("ld_w_last")
        s_ld_w3 = sem("ld_w_middle")
        s_x = [sem(f"x_loaded{n}") for n in range(4)]
        s_cwb = [sem(f"weights_bcast{n}") for n in range(2)]
        s_shared = sem("shared_rows_stored")
        s_cwst = sem("cw_rows_stored")
        s_out = sem("out_stored")
        s_const, s_ones, s_siluc, s_silub, s_gt, s_wt_mm, s_wt_a, s_wt_d = (sem(n) for n in (
            "const", "ones", "siluc", "silub", "gate_chain", "wT_mm", "wT_act", "wT_dve"))
        s_mod1_mm, s_ga_mm, s_cols_mm, s_gb_mm = (sem(n) for n in (
            "mod1_mm", "gate_a_mm", "mod_cols_mm", "gate_b_mm"))
        s_mod1, s_ga_raw, s_ga, s_cols, s_gb_raw = (sem(n) for n in (
            "mod1", "gate_a_raw", "gate_a", "mod_cols", "gate_b_raw"))
        s_gb = sem("gate_b")
        s_wr0 = sem("router_pad_zeroed")
        s_table, s_eps = sem("act_table"), sem("eps")
        s_constr, s_wqk_mm, s_wvo_mm, s_wvo_raw, s_wvf = (sem(n) for n in (
            "const_r", "wqk_mm", "wvo_mm", "wvo_raw", "wvo_gated"))
        s_wqk_hi, s_wqk_lo, s_wvo_hi, s_wvo_lo, s_wr_hi, s_wr_lo = (sem(n) for n in (
            "wqk_hi", "wqk_lo", "wvo_hi", "wvo_lo", "router_w_hi", "router_w_lo"))
        tl = {n: sem("t_" + n) for n in (
            "bn1", "stat1", "u", "h", "bn2", "stat2", "xlo", "negmax", "vqlo", "ptlo", "rinv", "x1", "bn3", "stat3",
            "hlo",
            "eps1", "rstd1", "eps2", "rstd2", "shift2", "rmul", "resid", "eps3", "rstd3", "shift3", "z2",
            "xT", "vq", "scores", "pT", "h2T", "pv",
            "xn", "xf", "xhi", "exp", "vqhi", "pthi", "h2f", "hhi")}

        def done(eng, stage_, t):
            if t >= 0:
                eng.wait_ge(tl[stage_], t + 1)

        s_lgT_mm, s_lgT, s_lg_mm, s_lg = (sem(n) for n in ("logitsT_mm", "logitsT", "logits_mm", "logits_evac"))
        s_rt, s_rexp, s_cwT_mm, s_cwT = (sem(n) for n in ("router_chain", "router_exp", "cwT_mm", "cwT_evac"))
        s_whi, s_wlo, s_ab, s_y, s_silu, s_up, s_g, s_ghi, s_glo = (sem(n) for n in (
            "w_hi", "w_lo", "gate_up_mm", "down_mm", "silu", "up_mul", "g", "g_hi", "g_lo"))
        s_final_half = [sem(f"y_final_half{n}") for n in range(2)]
        s_ya, s_yd, s_yT_mm, s_gated, s_final = (sem(n) for n in (
            "y_evac_act", "y_evac_dve", "y_back", "y_gated", "y_final"))

        x_t = x.rearrange("b (i p) d -> b i p d", p=P)
        out_t = out.rearrange("b (n t p) d -> (b n) p t d", t=BT, p=P)

        def load_weights(eng, first, end, sem_):
            for c in range(DC):
                rows = slice(c * P, (c + 1) * P)
                for w, at in ((we1, W1), (we3, W3)):
                    eng.dma_start(w_raw[:, first:end, at + c * P:at + (c + 1) * P],
                                  w[first - SH:end - SH, rows, :].rearrange("e p h -> p e h")).then_inc(sem_, 16)
            eng.dma_start(w_raw[:, first:end, W2:WX],
                          we2[first - SH:end - SH].rearrange("e p d -> p e d")).then_inc(sem_, 16)

        block = ctx.enter_context(nc.Block())

        @block.sync
        def _(sp):
            with nc.allow_non_contiguous_dma(reason="small column loads"):
                sp.dma_start(cols[:, 2:2 + B, :], c_in.rearrange("b (c p) -> p b c", p=P)).then_inc(s_ld_c, 16)

            def token_tile(t):
                done(sp, "resid", t - 4)
                sp.dma_start(x_in[:, t % 4, :], x_t[t // NT, t % NT]).then_inc(s_x[t % 4], 16)

            sp.dma_start(qkv_sb, qkv.rearrange("(c p) n -> p c n", p=P)).then_inc(s_ld_qkv, 16)
            token_tile(0)
            with nc.allow_non_contiguous_dma(reason="small column loads"):
                sp.dma_start(cols[:, 0, :], gamma.rearrange("(c p) -> p c", p=P)).then_inc(s_ld_cols, 16)
                sp.dma_start(cols[:, 1, :], beta.rearrange("(c p) -> p c", p=P)).then_inc(s_ld_cols, 16)
            for t in range(1, 4):
                token_tile(t)
            sp.wait_ge(s_wr0, 1)
            sp.dma_start(wr_raw[:, :, 0:E], w_router.rearrange("(c p) e -> p c e", p=P)).then_inc(s_ld_wr, 16)
            for t in range(4, 6):
                token_tile(t)
            for c in range(DC):
                rows = slice(c * P, (c + 1) * P)
                sp.dma_start(w_raw[:, 0:SH, W1 + c * P:W1 + (c + 1) * P],
                             ws1[rows, :].rearrange("p (e h) -> p e h", h=H)).then_inc(s_ld_w, 16)
                sp.dma_start(w_raw[:, 0:SH, W3 + c * P:W3 + (c + 1) * P],
                             ws3[rows, :].rearrange("p (e h) -> p e h", h=H)).then_inc(s_ld_w, 16)
            sp.dma_start(w_raw[:, 0:SH, W2:WX], ws2.rearrange("(e p) d -> p e d", p=P)).then_inc(s_ld_w, 16)
            sp.dma_start(cw_dram[0:SH, :].rearrange("e (n t) -> e n t", t=P),
                         shared_row[:].rearrange("e (n t) -> e n t", n=1).broadcast_to((SH, T // P, P))
                         ).then_inc(s_shared, 16)
            for t in range(6, 8):
                token_tile(t)
            load_weights(sp, SH, EARLY, s_ld_w)
            for t in range(8, 10):
                token_tile(t)
            sp.wait_ge(s_cols_mm, 1)
            sp.wait_ge(s_gb_mm, 2)
            load_weights(sp, MID, EX, s_ld_w2)
            for t in range(10, TILES):
                token_tile(t)

            def weights(b, e, k, n):
                if not (isinstance(n, int) and n < 2):
                    sp.wait_ge(s_g, n - 2 + 1)
                row = cw_dram[e:e + 1, :] if isinstance(e, int) else cw_dram[bass.ds(e, 1), :]
                cut = row[:, b * TB:(b + 1) * TB] if isinstance(b, int) else row[:, bass.ds(b * TB, TB)]
                sp.dma_start(cwb[:, k % 2, :], cut.broadcast_to((P, TB))).then_inc(s_cwb[k % 2], 16)

            def store(b):
                sp.wait_ge(s_final, b + 1)
                dst = out_t[b] if isinstance(b, int) else out_t[bass.ds(b, 1)].rearrange("a p t d -> (a p) t d")
                sp.dma_start(dst, y_out).then_inc(s_out, 16)

            def group(b, g):
                for k in range(UN):
                    e = g * UN + k
                    weights(b, e, k, b * EX + e)

            sp.wait_ge(s_shared, 16)
            done(sp, "resid", TILES - 1)
            done(sp, "xT", TILES - 1)
            weights(0, 0, 0, 0)
            weights(0, 1, 1, 1)
            sp.wait_ge(s_cwT, 1)
            sp.dma_start(cw_dram[SH:EX, 0:S], cwT).then_inc(s_cwst, 16)
            weights(0, 2, 2, 2)
            weights(0, 3, 3, 3)
            done(sp, "pT", B * UNITS - 1)
            done(sp, "hlo", TILES - 1)
            load_weights(sp, EARLY, MID, s_ld_w3)
            sp.wait_ge(s_cwst, 16)
            with sp.Fori(1, PEELED) as g:
                group(0, g)
            sp.wait_ge(s_cwT, 2)
            sp.dma_start(cw_dram[SH:EX, S:T], cwT).then_inc(s_cwst, 16)
            with sp.Fori(PEELED, NG) as g:
                group(0, g)
            group(1, 0)
            with sp.Fori(1, NB - 1) as b:
                group(b, 1)
                store(b - 1)
                with sp.Fori(2, NG) as g:
                    group(b, g)
                sp.wait_ge(s_cwst, 32)
                group(b + 1, 0)
            group(NB - 1, 1)
            store(NB - 2)
            with sp.Fori(2, NG) as g:
                group(NB - 1, g)
            for half in range(2):
                sp.wait_ge(s_final_half[half], 1)
                rows = slice(half * BT // 2, (half + 1) * BT // 2)
                sp.dma_start(out_t[NB - 1, :, rows, :], y_out[:, rows, :]).then_inc(s_out, 16)
            sp.wait_ge(s_out, 16 * (NB + 1))

        @block.gpsimd
        def _(pool):
            nc.gpsimd.memset(eps[:], EPS).then_inc(s_eps, 1)
            nc.gpsimd.memset(ident[:], 1.0).then_inc(s_const, 1)
            nc.gpsimd.memset(mask_raw, 0.0).then_inc(s_const, 1)
            nc.gpsimd.memset(minus_half[:], -0.5).then_inc(s_const, 1)
            nc.gpsimd.memset(shared_row[:], 1.0 / (TOPK + 1)).then_inc(s_const, 1)
            nc.gpsimd.memset(wr_raw, 0.0).then_inc(s_wr0, 1)
            pool.wait_ge(s_const, 4)
            pool.wait_ge(s_eps, 1)
            nc.gpsimd.affine_select(out=ident[:], in_=ident[:], compare_op=ALU.is_equal, fill=0.0, base=0,
                                    pattern=[[-1, P]], channel_multiplier=1).then_inc(s_const, 1)
            nc.gpsimd.affine_select(out=mask_raw, in_=mask_raw, compare_op=ALU.is_ge, fill=MASKED,
                                    base=0, pattern=[[-1, P]], channel_multiplier=1).then_inc(s_const, 1)

            def inverse_std(n, t, read_by):
                v, r = veps[:, n - 1, t % 4:t % 4 + 1], rstd[:, n - 1, t % 4:t % 4 + 1]
                done(pool, f"stat{n}", t)
                nc.gpsimd.tensor_tensor(v, mv[:, n - 1, t % 4, 1:2], eps[:], ALU.add).then_inc(tl[f"eps{n}"], 1)
                done(pool, f"eps{n}", t)
                done(pool, read_by, t - 4)
                nc.gpsimd.tensor_tensor(r, v, minus_half[:], ALU.pow).then_inc(tl[f"rstd{n}"], 1)

            def mean_shift(n, t):
                done(pool, f"rstd{n}", t)
                nc.gpsimd.tensor_scalar(shift[:, n - 1, t % 4:t % 4 + 1], mv[:, n - 1, t % 4, 0:1],
                                        rstd[:, n - 1, t % 4:t % 4 + 1], -1.0, ALU.mult, ALU.mult
                                        ).then_inc(tl[f"shift{n}"], 1)

            def norm_of_h(t):
                inverse_std(2, t, "xn")
                mean_shift(2, t)

            def residual(t):
                done(pool, "h", t)
                if t % NT == 0:
                    pool.wait_ge(s_ga, t // NT + 1)
                nc.gpsimd.tensor_tensor(x1[:, t, :], h[:, t % 2, :], mod[:, t // NT, 2 * D:3 * D], ALU.mult
                                        ).then_inc(tl["rmul"], 1)
                done(pool, "rmul", t)
                nc.gpsimd.tensor_tensor(x1[:, t, :], x1[:, t, :], x_in[:, t % 4, :], ALU.add
                                        ).then_inc(tl["resid"], 1)

            def norm2(t):
                inverse_std(3, t, "z2")
                mean_shift(3, t)
                done(pool, "shift3", t)
                done(pool, "h2T", t - 2)
                nc.gpsimd.tensor_scalar(z2[:, t % 2, :], x1[:, t, :], rstd[:, 2, t % 4:t % 4 + 1],
                                        shift[:, 2, t % 4:t % 4 + 1], ALU.mult, ALU.add).then_inc(tl["z2"], 1)

            def split_lo(e, k, n):
                pool.wait_ge(s_whi, n + 1)
                src = w_raw_of(e)
                pool.nop(nofuse=True)
                nc.gpsimd.tensor_tensor(w_lo[k], src, w_hi[k].bitcast(F32), ALU.subtract
                                        ).then_inc(s_wlo, 1)

            for s in range(FIRST, LAST + 1):
                if 0 <= s - 2:
                    norm2(s - 2)
                if s == LAST - 1:
                    split_lo(0, 0, 0)
                    split_lo(1, 1, 1)
                if s == LAST:
                    split_lo(2, 2, 2)
                    split_lo(3, 3, 3)
                if 0 <= s + 3 < TILES:
                    residual(s + 3)
                if s + 5 < TILES:
                    inverse_std(1, s + 5, "h")
                if 0 <= s + 4 < TILES:
                    norm_of_h(s + 4)

            def finish(b):
                pool.wait_ge(s_gated, b + 1)
                x1_b = (x1[:, b * BT:(b + 1) * BT, :] if isinstance(b, int)
                        else x1[:, bass.ds(b * BT, BT), :])
                pool.nop(nofuse=True)
                nc.gpsimd.tensor_tensor(y_out, y_out, x1_b, ALU.add).then_inc(s_final, 1)

            def group(b, g, static=False, last=False):
                for k in range(UN):
                    e = g * UN + k + 2
                    if static and e >= EX:
                        if not last:
                            split_lo(e - EX, (k + 2) % UN, b * EX + e)
                    else:
                        split_lo(e, (k + 2) % UN, b * EX + e)

            def rest(b, first=1, last=False):
                with pool.Fori(first, NG - 1) as g:
                    group(b, g)
                group(b, NG - 1, static=True, last=last)

            norm2(TILES - 1)
            for n in range(UN, UN + 2):
                split_lo(n, n % UN, n)
            group(0, 1, static=True)
            rest(0, first=2)
            group(1, 0, static=True)
            finish(0)
            with pool.Fori(1, NB - 1) as b:
                rest(b)
                group(b + 1, 0, static=True)
                finish(b)
            rest(NB - 1, last=True)
            pool.wait_ge(s_gated, NB)
            nc.gpsimd.tensor_tensor(y_out[:, 0:BT // 2, :], y_out[:, 0:BT // 2, :],
                                    x1[:, TILES - BT:TILES - BT // 2, :], ALU.add).then_inc(s_final_half[0], 1)

        @block.scalar
        def _(act):
            def load_modulation(n):
                act.dma_start(wmod_sb[:, :, 2 * n * D:2 * (n + 1) * D],
                              wmod[:, 2 * n * D:2 * (n + 1) * D].rearrange("(c p) n -> p c n", p=P)
                              ).then_inc(s_ld_wmod[n], 16)

            tables = [0]

            def load_table(func):
                act.wait_ge(s_eps, 1)
                if tables[0]:
                    act.wait_ge(s_table, tables[0])
                nc.scalar.activation(table_out[:], eps[:], func).then_inc(s_table, 1)
                tables[0] += 1

            load_modulation(0)
            load_modulation(1)
            load_table(ACT.Silu)
            act.wait_ge(s_ld_c, 16)
            nc.scalar.activation(silu_c[:], cols[:, 2:4, :], ACT.Silu).then_inc(s_siluc, 1)
            act.dma_start(o_sb, o_proj.rearrange("(c p) n -> p c n", p=P)).then_inc(s_ld_o, 16)
            load_modulation(2)
            act.wait_ge(s_const, 6)
            nc.scalar.activation(ident_r[:], ident[:], ACT.Copy).then_inc(s_constr, 1)
            nc.scalar.activation(mask_r[:], mask_raw, ACT.Copy).then_inc(s_constr, 1)
            act.wait_ge(s_wt_mm, 1)
            nc.scalar.activation(wT_sb[:, 0, :, :], ps[:, 6, :].rearrange("p (k c) -> p k c", k=DC), ACT.Copy
                                 ).then_inc(s_wt_a, 1)
            act.wait_ge(s_wt_mm, 3)
            nc.scalar.activation(wT_sb[:, 2, :, :], ps[:, 5, :].rearrange("p (k c) -> p k c", k=DC), ACT.Copy
                                 ).then_inc(s_wt_a, 1)
            act.wait_ge(s_wqk_mm, 1)
            nc.scalar.activation(wqk_hi, ps[:, 6, :].rearrange("p (c d) -> p c d", c=DC), ACT.Copy,
                                 scale=D ** -0.5).then_inc(s_wqk_hi, 1)

            def wvo_copy():
                act.wait_ge(s_wvo_mm, 1)
                nc.scalar.activation(wT_sb[:, 2, :, :], ps[:, 7, :].rearrange("p (c d) -> p c d", c=DC), ACT.Copy
                                     ).then_inc(s_wvo_raw, 1)

            def wvo_split(b):
                act.wait_ge(s_wvf, b + 1)
                nc.scalar.activation(wvo_hi[:, b, :, :], wT_sb[:, b, :, :], ACT.Copy).then_inc(s_wvo_hi, 1)

            def gate_a_copy():
                act.wait_ge(s_ga_mm, 2)
                nc.scalar.activation(mod[:, 1, 2 * D:3 * D], ps[:, 3, 0:D], ACT.Copy).then_inc(s_ga_raw, 1)

            def gate_b_copy():
                act.wait_ge(s_gb_mm, 2)
                nc.scalar.activation(gate_b[:, 0:NB:2, :], ps[:, 5, :].rearrange("p (b d) -> p b d", b=B), ACT.Copy
                                     ).then_inc(s_gb_raw, 1)

            def router_weights():
                act.wait_ge(s_ld_wr, 16)
                nc.scalar.activation(wr_hi[:], wr_raw, ACT.Copy).then_inc(s_wr_hi, 1)

            def split_hi(e, k, n):
                if not (isinstance(n, int) and n < UN):
                    act.wait_ge(s_y, n - UN + 1)
                src = w_raw_of(e)
                nc.scalar.activation(w_hi[k], src, ACT.Copy).then_inc(s_whi, 1)

            def silu_step(k, n):
                act.wait_ge(s_ab, n + 1)
                if not (isinstance(n, int) and n < 2):
                    act.wait_ge(s_glo, n - 2 + 1)
                else:
                    done(act, "resid", TILES - 1)
                nc.scalar.activation(act_g[:, k % 2, :], ps[:, 2 * (k % 2), :], ACT.Silu).then_inc(s_silu, 1)

            def router_exp(row):
                act.wait_ge(s_rt, row * R_ROW + R_SHIFTED)
                nc.scalar.activation(cw, cw, ACT.Exp).then_inc(s_rexp, 1)

            def cw_evac(row):
                act.wait_ge(s_cwT_mm, row + 1)
                nc.scalar.activation(cwT, ps[0:E, TR:TR + 2, :].rearrange("p b n -> p (b n)"), ACT.Copy
                                     ).then_inc(s_cwT, 1)

            def norm2_hi(t):
                done(act, "h2T", t)
                done(act, "hlo", t - 2)
                if t == 0:
                    act.wait_ge(s_cols, 1)
                for c in range(DC):
                    last = nc.scalar.activation(h2f[:, t % 2, c, :], ps[:, Y0, c * P:(c + 1) * P], ACT.Identity,
                                                scale=mod_cols[:, t // NT, 1, c:c + 1],
                                                bias=mod_cols[:, t // NT, 0, c:c + 1])
                last.then_inc(tl["h2f"], 1)
                done(act, "h2f", t)
                nc.scalar.activation(h2T_hi[:, :, t * P:(t + 1) * P], h2f[:, t % 2, :, :], ACT.Copy
                                     ).then_inc(tl["hhi"], 1)

            for s in range(FIRST, LAST + 1):
                if s == -2:
                    wvo_copy()
                if s == 2:
                    gate_b_copy()
                if s == 6:
                    wvo_split(1)
                    router_weights()
                if s == LAST:
                    silu_step(0, 0)
                t = s - 1
                if 0 <= t < TILES:
                    for u, first, n in units_of(t):
                        done(act, "pT", u)
                        if u >= PT_RING:
                            done(act, "pv", tile_of_unit(u - PT_RING))
                        nc.scalar.activation(pT_hi[:, u % PT_RING, 0:n * P], ps[:, X0 + u % 2, 0:n * P],
                                             ACT.Copy).then_inc(tl["pthi"], 1)
                t = s + 2
                if 0 <= t < TILES:
                    at = slot_of(t) * P
                    done(act, "xT", t)
                    if t == 0:
                        act.wait_ge(s_ld_cols, 32)
                    done(act, "xlo", t - 2)
                    for c in range(DC):
                        last = nc.scalar.activation(xf[:, t % 2, c, :], ps[:, Y0, c * P:(c + 1) * P], ACT.Identity,
                                                    scale=cols[:, 0, c:c + 1], bias=cols[:, 1, c:c + 1])
                    last.then_inc(tl["xf"], 1)
                    done(act, "xf", t)
                    if t >= KEY_SLOTS:
                        done(act, "scores", NT - 1)
                    nc.scalar.activation(xnT_hi[:, :, at:at + P], xf[:, t % 2, :, :], ACT.Copy
                                         ).then_inc(tl["xhi"], 1)
                if s == ROUTE + 4:
                    cw_evac(0)
                t = s
                if 0 <= t < TILES:
                    done(act, "negmax", t)
                    if t >= 2:
                        done(act, "pT", units_of(t - 2)[-1][0])
                    done(act, "rinv", t - 4)
                    nc.scalar.activation(probs[:, t % 2, 0:(t % NT + 1) * P], score_banks(t), ACT.Exp,
                                         bias=negmax[:, t % 4:t % 4 + 1],
                                         accum_out=rowsum[:, t % 4:t % 4 + 1]).then_inc(tl["exp"], 1)
                t = s + 1
                if 0 <= t < TILES:
                    done(act, "vq", t)
                    done(act, "scores", t - 2)
                    if t >= KEY_SLOTS:
                        done(act, "pv", NT - 1)
                    nc.scalar.activation(vq(V_HI, Q_HI, t), ps[:, Y1, :].rearrange("p (two x) -> p two x", two=2),
                                         ACT.Copy).then_inc(tl["vqhi"], 1)
                if s == -2:
                    wvo_split(0)
                    gate_a_copy()
                    load_table(ACT.Exp)
                if 0 <= s - 2 < TILES:
                    norm2_hi(s - 2)
                t = s + 3
                if 0 <= t < TILES:
                    done(act, "shift2", t)
                    done(act, "xT", t - 2)
                    nc.scalar.activation(xn[:, t % 2, :], h[:, t % 2, :], ACT.Identity,
                                         scale=rstd[:, 1, t % 4:t % 4 + 1], bias=shift[:, 1, t % 4:t % 4 + 1]
                                         ).then_inc(tl["xn"], 1)
                if ROUTE - 1 <= s <= ROUTE:
                    half = s - (ROUTE - 1)
                    act.wait_ge(s_lgT_mm, half + 1)
                    nc.scalar.activation(logitsT[:, half * TB:(half + 1) * TB], ps[0:E, 2 * half + 1, :], ACT.Copy
                                         ).then_inc(s_lgT, 1)
                if s == ROUTE + 2:
                    router_exp(0)
                if s == LAST - 2:
                    act.wait_ge(s_ld_w, 10 * 16)
                    done(act, "vqlo", TILES - 1)
                    split_hi(0, 0, 0)
                    split_hi(1, 1, 1)
                if s == LAST - 1:
                    split_hi(2, 2, 2)
                    split_hi(3, 3, 3)
                    load_table(ACT.Silu)

            def g_hi_step(k, n):
                act.wait_ge(s_g, n + 1)
                if not (isinstance(n, int) and n < 2):
                    act.wait_ge(s_y, n - 2 + 1)
                nc.scalar.activation(g_hi[:, k % 2, :], act_g[:, k % 2, :], ACT.Copy).then_inc(s_ghi, 1)

            def evac(b):
                act.wait_ge(s_y, b * EX + EX)
                if not (isinstance(b, int) and b == 0):
                    act.wait_ge(s_yT_mm, b)
                nc.scalar.activation(yT[:, 0, :], ps[:, 4, :], ACT.Copy).then_inc(s_ya, 1)

            def group(b, g, static=False, evac_of=None, last=False):
                for k in range(UN):
                    n = b * EX + (g * UN + k)
                    silu_step(k, n)
                    e = g * UN + k + 2
                    if static and e >= EX:
                        if not last:
                            split_hi(e - EX, (k + 2) % UN, n + 2)
                    else:
                        split_hi(e, (k + 2) % UN, n + 2)
                    if k == 1 and evac_of is not None:
                        evac(evac_of)
                    g_hi_step(k, n)

            def rest(b, first=1, last=False):
                with act.Fori(first, NG - 1) as g:
                    group(b, g)
                group(b, NG - 1, static=True, last=last)

            def logits_row1():
                act.wait_ge(s_lgT_mm, 4)
                act.wait_ge(s_cwst, 16)
                nc.scalar.activation(logitsT, ps[0:E, TR:TR + 2, :].rearrange("p b n -> p (b n)"), ACT.Copy
                                     ).then_inc(s_lgT, 1)

            for n in range(PEELED * UN):
                if n > 0:
                    silu_step(n % UN, n)
                if n == 2:
                    norm2_hi(TILES - 1)
                if n == 3:
                    logits_row1()
                if n == 6:
                    router_exp(1)
                if n == 9:
                    cw_evac(1)
                if n + 2 == EARLY:
                    act.wait_ge(s_ld_w3, 5 * 16)
                if n + 2 >= UN:
                    split_hi(n + 2, (n + 2) % UN, n + 2)
                g_hi_step(n % UN, n)
            act.wait_ge(s_ld_w2, 5 * 16)
            rest(0, first=PEELED)
            act.wait_ge(s_cwst, 32)
            group(1, 0, static=True, evac_of=0)
            with act.Fori(1, NB - 1) as b:
                rest(b)
                group(b + 1, 0, static=True, evac_of=b)
            rest(NB - 1, last=True)
            evac(NB - 1)

        @block.vector
        def _(dve):
            nc.vector.memset(silu_b, 1.0).then_inc(s_ones, 1)
            dve.wait_ge(s_ones, 1)
            dve.wait_ge(s_siluc, 1)
            for b in range(B):
                for c in range(DC):
                    nc.vector.tensor_scalar(silu_b[:, b, c, :], silu_b[:, b, c, :], silu_c[:, b, c:c + 1], None,
                                            ALU.mult).then_inc(s_silub, 1)
            dve.wait_ge(s_wt_mm, 2)
            nc.vector.tensor_copy(wT_sb[:, 1, :, :], ps[:, 7, :].rearrange("p (k c) -> p k c", k=DC)
                                  ).then_inc(s_wt_d, 1)

            def modulation1(b):
                dve.wait_ge(s_mod1_mm, b + 1)
                nc.vector.tensor_copy(mod[:, b, 0:D], ps[:, b, 0:D]).then_inc(s_mod1, 1)
                nc.vector.tensor_scalar(mod[:, b, D:2 * D], ps[:, b, D:2 * D], 1.0, None, ALU.add
                                        ).then_inc(s_mod1, 1)

            gates = [0]

            def gate(dst, src, tmp):
                def then(ins):
                    gates[0] += 1
                    ins.then_inc(s_gt, 1)

                then(nc.vector.tensor_scalar(tmp, src, 0.0, 2.0, ALU.is_ge, ALU.mult))
                if src is not dst:
                    then(nc.vector.tensor_copy(dst, src))
                dve.wait_ge(s_gt, gates[0])
                then(nc.vector.scalar_tensor_tensor(out=dst, in0=dst, scalar=-1.0, in1=dst, op0=ALU.mult,
                                                    op1=ALU.max))
                dve.wait_ge(s_gt, gates[0])
                then(nc.vector.tensor_scalar(dst, dst, GATE_FLOOR, None, ALU.max))
                dve.wait_ge(s_gt, gates[0])
                return nc.vector.scalar_tensor_tensor(out=dst, in0=tmp, scalar=-1.0, in1=dst, op0=ALU.add,
                                                      op1=ALU.mult)

            def gate_a(b):
                dst = mod[:, b, 2 * D:3 * D]
                if b == 0:
                    dve.wait_ge(s_ga_mm, 1)
                    gate(dst, ps[:, 2, 0:D], gate_tmp).then_inc(s_ga, 1)
                else:
                    dve.wait_ge(s_ga_raw, 1)
                    dve.wait_ge(s_ga, 1)
                    gate(dst, dst, gate_tmp).then_inc(s_ga, 1)

            def wqk_split():
                dve.wait_ge(s_wqk_hi, 1)
                nc.vector.scalar_tensor_tensor(out=wqk_lo, in0=ps[:, 6, :].rearrange("p (c d) -> p c d", c=DC),
                                               scalar=D ** -0.5, in1=wqk_hi.bitcast(F32), op0=ALU.mult,
                                               op1=ALU.subtract).then_inc(s_wqk_lo, 1)

            def wvo_gate(b):
                dve.wait_ge(s_wvo_raw, 1)
                dve.wait_ge(s_ga, b + 1)
                for c in range(DC):
                    last = nc.vector.tensor_tensor(wT_sb[:, b, c, :], wT_sb[:, 2, c, :], mod[:, b, 2 * D:3 * D],
                                                   ALU.mult)
                last.then_inc(s_wvf, 1)

            def wvo_split(b):
                dve.wait_ge(s_wvo_hi, b + 1)
                nc.vector.tensor_tensor(wvo_lo[:, b, :, :], wT_sb[:, b, :, :], wvo_hi[:, b, :, :].bitcast(F32),
                                        ALU.subtract).then_inc(s_wvo_lo, 1)

            def modulation2():
                dve.wait_ge(s_cols_mm, 1)
                for half in range(2):
                    for c in range(DC):
                        src = ps[:, 4, (half * DC + c) * B:(half * DC + c + 1) * B]
                        last = nc.vector.tensor_scalar(mod_cols[:, :, half, c], src, float(half), None, ALU.add)
                last.then_inc(s_cols, 1)

            def gate_b_chain():
                dve.wait_ge(s_gb_raw, 1)
                one, two = gate_b[:, 0:NB:2, :], gate_b[:, 1:NB:2, :]
                gate(one, one, two).then_inc(s_gb, 1)
                dve.wait_ge(s_gb, 1)
                nc.vector.tensor_copy(two, one).then_inc(s_gb, 1)

            def router_weights():
                dve.wait_ge(s_wr_hi, 1)
                nc.vector.tensor_tensor(wr_lo[:], wr_raw, wr_hi[:].bitcast(F32), ALU.subtract).then_inc(s_wr_lo, 1)

            def stats(n, src, t):
                done(dve, f"stat{n}", t - 4)
                nc.vector.bn_stats(bn[:, n - 1, t % 4, :], src).then_inc(tl[f"bn{n}"], 1)

            def stats_end(n, t, *read_by):
                done(dve, f"bn{n}", t)
                for stage_ in read_by:
                    done(dve, stage_, t - 4)
                nc.vector.bn_aggr(mv[:, n - 1, t % 4, :], bn[:, n - 1, t % 4, :]).then_inc(tl[f"stat{n}"], 1)

            def x_lo(t):
                at = slot_of(t) * P
                done(dve, "xhi", t)
                nc.vector.tensor_tensor(xnT_lo[:, :, at:at + P], xf[:, t % 2, :, :],
                                        xnT_hi[:, :, at:at + P].bitcast(F32), ALU.subtract).then_inc(tl["xlo"], 1)

            def vq_lo(t):
                done(dve, "vqhi", t)
                nc.vector.tensor_tensor(vq(V_LO, Q_LO, t), ps[:, Y1, :].rearrange("p (two x) -> p two x", two=2),
                                        vq(V_HI, Q_HI, t).bitcast(F32), ALU.subtract).then_inc(tl["vqlo"], 1)

            def norm2_lo(t):
                done(dve, "hhi", t)
                nc.vector.tensor_tensor(h2T_lo[:, :, t * P:(t + 1) * P], h2f[:, t % 2, :, :],
                                        h2T_hi[:, :, t * P:(t + 1) * P].bitcast(F32), ALU.subtract
                                        ).then_inc(tl["hlo"], 1)

            chain = [0]

            def link(ins):
                chain[0] += 1
                ins.then_inc(s_rt, 1)

            def settle():
                dve.wait_ge(s_rt, chain[0])

            full = (P, NT, E)

            def route_top(row):
                lg = logits[:, row * NT:(row + 1) * NT, :]
                dve.wait_ge(s_lg_mm, row + 1)
                nc.vector.tensor_copy(lg, ps[:, Y0, 0:NT * E].rearrange("p (t e) -> p t e", e=E)).then_inc(s_lg, 1)
                dve.wait_ge(s_lg, row + 1)
                for t in range(NT):
                    link(nc.vector.max(top8[:, t, :], lg[:, t, :]))
                settle()
                dve.wait_ge(s_cwT_mm, row)
                link(nc.vector.tensor_tensor(cw, lg, top8[:, :, 0:1].broadcast_to(full), ALU.subtract))
                assert chain[0] == row * R_ROW + R_SHIFTED

            def route_select(row):
                lg = logits[:, row * NT:(row + 1) * NT, :]
                fourth = top8[:, :, TOPK - 1:TOPK].broadcast_to(full)
                link(nc.vector.tensor_tensor(above, lg, fourth, ALU.is_gt))
                link(nc.vector.tensor_tensor(ties, lg, fourth, ALU.is_equal))
                link(nc.vector.memset(reset, 1.0))
                settle()
                link(nc.vector.memset(reset[:, :, 0:1], 0.0))
                link(nc.vector.tensor_reduce(need, above, AX.X, ALU.add))
                settle()
                link(nc.vector.tensor_scalar(need, need, -1.0, float(TOPK), ALU.mult, ALU.add))
                link(nc.vector.tensor_tensor_scan(nth_tie.rearrange("p t e -> p (t e)"),
                                                  reset.rearrange("p t e -> p (t e)"),
                                                  ties.rearrange("p t e -> p (t e)"), 0.0, ALU.mult, ALU.add))
                settle()
                link(nc.vector.tensor_tensor(nth_tie, nth_tie, need.broadcast_to(full), ALU.is_le))
                settle()
                link(nc.vector.tensor_tensor(ties, ties, nth_tie, ALU.mult))
                settle()
                link(nc.vector.tensor_tensor(ties, ties, above, ALU.add))

            def route_weights(row):
                settle()
                dve.wait_ge(s_rexp, row + 1)
                link(nc.vector.tensor_tensor(cw, cw, ties, ALU.mult))
                settle()
                link(nc.vector.tensor_reduce(total, cw, AX.X, ALU.add))
                settle()
                link(nc.vector.reciprocal(total, total))
                settle()
                link(nc.vector.tensor_scalar(total, total, TOPK / (TOPK + 1.0), None, ALU.mult))
                settle()
                link(nc.vector.tensor_tensor(cw, cw, total.broadcast_to(full), ALU.mult))
                assert chain[0] == (row + 1) * R_ROW

            def step(k, n, slot_round, between=None):
                dve.wait_ge(s_silu, n + 1)
                nc.vector.tensor_tensor(act_g[:, k % 2, :], act_g[:, k % 2, :], ps[:, 2 * (k % 2) + 1, :],
                                        ALU.mult).then_inc(s_up, 1)
                dve.wait_ge(s_up, n + 1)
                dve.wait_ge(s_cwb[k % 2], slot_round * 16)
                nc.vector.tensor_tensor(act_g[:, k % 2, :], act_g[:, k % 2, :], cwb[:, k % 2, :], ALU.mult
                                        ).then_inc(s_g, 1)
                if between is not None:
                    between()
                dve.wait_ge(s_ghi, n + 1)
                if not (isinstance(n, int) and n < 2):
                    dve.wait_ge(s_y, n - 2 + 1)
                nc.vector.tensor_tensor(g_lo[:, k % 2, :], act_g[:, k % 2, :], g_hi[:, k % 2, :].bitcast(F32),
                                        ALU.subtract).then_inc(s_glo, 1)

            for s in range(FIRST, LAST + 1):
                if s == -4:
                    modulation1(0)
                if s == -3:
                    wqk_split()
                    gate_a(0)
                    wvo_gate(0)
                if s == -1:
                    modulation2()
                if s == 7:
                    wvo_split(1)
                    router_weights()
                t = s - 1
                if 0 <= t < TILES:
                    for u, first, n in units_of(t):
                        done(dve, "pthi", u)
                        nc.vector.tensor_tensor(pT_lo[:, u % PT_RING, 0:n * P], ps[:, X0 + u % 2, 0:n * P],
                                                pT_hi[:, u % PT_RING, 0:n * P].bitcast(F32), ALU.subtract
                                                ).then_inc(tl["ptlo"], 1)
                t = s
                if 0 <= t < TILES:
                    done(dve, "scores", t)
                    done(dve, "exp", t - 4)
                    nc.vector.tensor_reduce(negmax[:, t % 4:t % 4 + 1], score_banks(t), AX.X, ALU.max,
                                            negate=True).then_inc(tl["negmax"], 1)
                a, c = s + 5, s + 4
                if a < TILES:
                    dve.wait_ge(s_x[a % 4], (a // 4 + 1) * 16)
                    stats(1, x_in[:, a % 4, :], a)
                if s == -2:
                    x_lo(0)
                    wvo_split(0)
                if s == -1:
                    x_lo(1)
                    vq_lo(0)
                if 0 <= c < TILES:
                    done(dve, "stat1", c)
                    done(dve, "resid", c - 2)
                    done(dve, "xn", c - 2)
                    if c % NT == 0:
                        dve.wait_ge(s_mod1, 2 * (c // NT + 1))
                    nc.vector.scalar_tensor_tensor(out=h[:, c % 2, :], in0=x_in[:, c % 4, :],
                                                   scalar=mv[:, 0, c % 4, 0:1], in1=mod[:, c // NT, D:2 * D],
                                                   op0=ALU.subtract, op1=ALU.mult).then_inc(tl["u"], 1)
                if a < TILES:
                    stats_end(1, a, "u", "eps1")
                if 0 <= s + 2 < TILES and s > -1:
                    x_lo(s + 2)
                if 0 <= c < TILES:
                    done(dve, "rstd1", c)
                    done(dve, "u", c)
                    nc.vector.scalar_tensor_tensor(out=h[:, c % 2, :], in0=h[:, c % 2, :],
                                                   scalar=rstd[:, 0, c % 4:c % 4 + 1], in1=mod[:, c // NT, 0:D],
                                                   op0=ALU.mult, op1=ALU.add).then_inc(tl["h"], 1)
                t = s - 1
                if 0 <= t < TILES:
                    done(dve, "exp", t)
                    done(dve, "x1", t - 4)
                    nc.vector.reciprocal(rinv[:, t % 4:t % 4 + 1], rowsum[:, t % 4:t % 4 + 1]
                                         ).then_inc(tl["rinv"], 1)
                if 0 <= s + 1 < TILES and s != -1:
                    vq_lo(s + 1)
                if 0 <= c < TILES:
                    done(dve, "h", c)
                    stats(2, h[:, c % 2, :], c)
                if s == LAST:
                    step(0, 0, 1, lambda: norm2_lo(TILES - 2))
                t = s - 1
                if 0 <= t < TILES:
                    done(dve, "rinv", t)
                    done(dve, "resid", t)
                    done(dve, "pv", t)
                    nc.vector.scalar_tensor_tensor(out=x1[:, t, :], in0=pv_out(t),
                                                   scalar=rinv[:, t % 4:t % 4 + 1], in1=x1[:, t, :],
                                                   op0=ALU.mult, op1=ALU.add).then_inc(tl["x1"], 1)
                if 0 <= c < TILES:
                    stats_end(2, c, "shift2")
                if 0 <= t < TILES:
                    done(dve, "x1", t)
                    stats(3, x1[:, t, :], t)
                if 0 <= s - 2 < TILES and s < LAST:
                    norm2_lo(s - 2)
                if 0 <= t < TILES:
                    stats_end(3, t, "shift3")
                if s == 0:
                    modulation1(1)
                if s == 4:
                    gate_a(1)
                if s == 5:
                    wvo_gate(1)
                if s == ROUTE + 1:
                    route_top(0)
                if s == ROUTE + 2:
                    route_select(0)
                if s == ROUTE + 3:
                    route_weights(0)

            def evac(b):
                dve.wait_ge(s_y, b * EX + EX)
                if not (isinstance(b, int) and b == 0):
                    dve.wait_ge(s_yT_mm, b)
                nc.vector.tensor_copy(yT[:, 1, :], ps[:, 5, :]).then_inc(s_yd, 1)

            def gated(b):
                dve.wait_ge(s_yT_mm, b + 1)
                if not (isinstance(b, int) and b == 0):
                    dve.wait_ge(s_out, b * 16)
                g_b = gate_b[:, b:b + 1, :] if isinstance(b, int) else gate_b[:, bass.ds(b, 1), :]
                nc.vector.tensor_tensor(y_out, ps[:, TR:TR + 2, :].rearrange("p k (t d) -> p (k t) d", d=D),
                                        g_b.broadcast_to((P, BT, D)), ALU.mult).then_inc(s_gated, 1)

            def group(b, g, evac_of=None):
                for k in range(UN):
                    between = (lambda: evac(evac_of)) if k == 1 and evac_of is not None else None
                    step(k, b * EX + (g * UN + k), b * (EX // 2) + (g * 2 + (k // 2 + 1)), between)

            def rest(b, first=1):
                with dve.Fori(first, NG) as g:
                    group(b, g)

            for n in range(1, PEELED * UN):
                step(n % UN, n, n // 2 + 1, (lambda: norm2_lo(TILES - 1)) if n == 2 else None)
                if n == 4:
                    route_top(1)
                if n == 5:
                    route_select(1)
                if n == 6:
                    route_weights(1)
                if n == 9:
                    gate_b_chain()
            rest(0, first=PEELED)
            dve.wait_ge(s_cwst, 32)
            group(1, 0, evac_of=0)
            gated(0)
            with dve.Fori(1, NB - 1) as b:
                rest(b)
                group(b + 1, 0, evac_of=b)
                gated(b)
            rest(NB - 1)
            evac(NB - 1)
            dve.wait_ge(s_out, (NB - 1) * 16)
            for half in range(2):
                rows = slice(half * BT // 2, (half + 1) * BT // 2)
                dve.wait_ge(s_yT_mm, NB + half)
                nc.vector.tensor_tensor(y_out[:, rows, :], ps[:, TR + half, :].rearrange("p (t d) -> p t d", d=D),
                                        gate_b[:, NB - 1:NB, :].broadcast_to((P, BT // 2, D)), ALU.mult
                                        ).then_inc(s_gated, 1)
            dve.wait_ge(s_gated, NB + 1)
            nc.vector.tensor_tensor(y_out[:, rows, :], y_out[:, rows, :], x1[:, TILES - BT // 2:TILES, :], ALU.add
                                    ).then_inc(s_final_half[1], 1)

        @block.tensor
        def _(pe):
            def split3(dst, w, x_, first, last):
                nc.tensor.matmul(dst, w[0], x_[0], start=first, stop=False)
                nc.tensor.matmul(dst, w[0], x_[1], start=False, stop=False)
                return nc.tensor.matmul(dst, w[1], x_[0], start=False, stop=last)

            def modulation(dst, n0, n1, b):
                for c in range(DC):
                    last = nc.tensor.matmul(dst, silu_b[:, b, c, :], wmod_sb[:, c, n0:n1], start=(c == 0),
                                            stop=(c == DC - 1))
                return last

            pe.wait_ge(s_silub, 2)
            pe.wait_ge(s_ld_wmod[0], 16)
            modulation(ps[:, 0, :], 0, 2 * D, 0).then_inc(s_mod1_mm, 1)
            pe.wait_ge(s_const, 6)
            pe.wait_ge(s_ld_qkv, 16)
            for m, bank in ((0, 6), (1, 7), (2, 5)):
                for k in range(DC):
                    for c in range(DC):
                        last = nc.tensor.transpose(ps[:, bank, k * D + c * P:k * D + (c + 1) * P],
                                                   qkv_sb[:, c, m * D + k * P:m * D + (k + 1) * P], ident[:])
                last.then_inc(s_wt_mm, 1)
            pe.wait_ge(s_wt_a, 1)
            pe.wait_ge(s_wt_d, 1)
            for c in range(DC):
                for k in range(DC):
                    last = nc.tensor.matmul(ps[:, 6, c * D:(c + 1) * D], wT_sb[:, 0, k, c * P:(c + 1) * P],
                                            wT_sb[:, 1, k, :], start=(k == 0), stop=(k == DC - 1))
            last.then_inc(s_wqk_mm, 1)
            pe.wait_ge(s_ld_wmod[1], 16)
            modulation(ps[:, 2, 0:D], 2 * D, 3 * D, 0).then_inc(s_ga_mm, 1)
            pe.wait_ge(s_wt_a, 2)
            pe.wait_ge(s_ld_o, 16)
            for c in range(DC):
                for k in range(DC):
                    last = nc.tensor.matmul(ps[:, 7, c * D:(c + 1) * D], wT_sb[:, 2, k, c * P:(c + 1) * P],
                                            o_sb[:, k, :], start=(k == 0), stop=(k == DC - 1))
            last.then_inc(s_wvo_mm, 1)

            def modulation1():
                pe.wait_ge(s_silub, 4)
                modulation(ps[:, 1, :], 0, 2 * D, 1).then_inc(s_mod1_mm, 1)

            def gate_a():
                modulation(ps[:, 3, 0:D], 2 * D, 3 * D, 1).then_inc(s_ga_mm, 1)

            def modulation2():
                pe.wait_ge(s_ld_wmod[2], 16)
                for half in range(2):
                    for m in range(DC):
                        n0 = (3 + half) * D + m * P
                        for c in range(DC):
                            last = nc.tensor.matmul(ps[:, 4, (half * DC + m) * B:(half * DC + m + 1) * B],
                                                    wmod_sb[:, c, n0:n0 + P], silu_c[:, :, c],
                                                    start=(c == 0), stop=(c == DC - 1))
                last.then_inc(s_cols_mm, 1)

            def gate_b(b):
                modulation(ps[:, 5, b * D:(b + 1) * D], 5 * D, 6 * D, b).then_inc(s_gb_mm, 1)

            def transpose_back(t):
                done(pe, "z2", t)
                done(pe, "xf", min(t + 4, TILES - 1))
                done(pe, "h2f", t - 1)
                for c in range(DC):
                    last = nc.tensor.transpose(ps[:, Y0, c * P:(c + 1) * P], z2[:, t % 2, c * P:(c + 1) * P],
                                               ident[:])
                last.then_inc(tl["h2T"], 1)

            def logits_half(row, half, bank):
                pe.wait_ge(s_wr_lo, 1)
                done(pe, "hlo", row * NT + (half + 1) * BT - 1)
                tok = slice(row * S + half * TB, row * S + (half + 1) * TB)
                for c in range(DC):
                    last = split3(ps[:, bank, :], (wr_hi[:, c, :], wr_lo[:, c, :]),
                                  (h2T_hi[:, c, tok], h2T_lo[:, c, tok]), c == 0, c == DC - 1)
                last.then_inc(s_lgT_mm, 1)

            def logits_back(row):
                pe.wait_ge(s_lgT, 2 + row)
                for t in range(NT):
                    last = nc.tensor.transpose(ps[:, Y0, t * E:(t + 1) * E], logitsT[:, t * P:(t + 1) * P],
                                               ident[0:E, 0:E])
                last.then_inc(s_lg_mm, 1)

            def cw_rows(row):
                if row == 0:
                    done(pe, "h2f", TILES - 4)
                    done(pe, "vqlo", TILES - 1)
                pe.wait_ge(s_rt, (row + 1) * R_ROW)
                for t in range(NT):
                    last = nc.tensor.transpose(ps[0:E, TR + t // BT, (t % BT) * P:(t % BT + 1) * P], cw[:, t, :],
                                               ident[:])
                last.then_inc(s_cwT_mm, 1)

            def gate_up(b, k, n):
                pe.wait_ge(s_wlo, n + 1)
                if not (isinstance(n, int) and n < 2):
                    pe.wait_ge(s_up, n - 2 + 1)
                elif n == 1:
                    done(pe, "exp", TILES - 1)
                tok = slice(b * TB, (b + 1) * TB) if isinstance(b, int) else bass.ds(b * TB, TB)
                for bank, at_ in ((2 * (k % 2), W1), (2 * (k % 2) + 1, W3)):
                    if at_ == W3 and isinstance(n, int) and n == 0:
                        done(pe, "x1", TILES - 2)
                    for c in range(DC):
                        cols_ = slice(at_ + c * P, at_ + (c + 1) * P)
                        last = split3(ps[:, bank, :], (w_hi[k][:, cols_], w_lo[k][:, cols_]),
                                      (h2T_hi[:, c, tok], h2T_lo[:, c, tok]), c == 0, c == DC - 1)
                last.then_inc(s_ab, 1)

            for s in range(FIRST, LAST + 1):
                if s == -1:
                    modulation1()
                    gate_a()
                    modulation2()
                if s == 0:
                    gate_b(0)
                if s == 1:
                    gate_b(1)
                t = s - 1
                if 0 <= t < TILES:
                    if t == 0:
                        pe.wait_ge(s_cols, 1)
                    if t == 1:
                        pe.wait_ge(s_gb_raw, 1)
                    done(pe, "exp", t)
                    for u, first, n in units_of(t):
                        done(pe, "ptlo", u - 2)
                        for j in range(n):
                            last = nc.tensor.transpose(ps[:, X0 + u % 2, j * P:(j + 1) * P],
                                                       probs[:, t % 2, (first + j) * P:(first + j + 1) * P], ident[:])
                        last.then_inc(tl["pT"], 1)
                if ROUTE - 1 <= s <= ROUTE:
                    half = s - (ROUTE - 1)
                    done(pe, "x1", NT - 2 + half)
                    logits_half(0, half, 2 * half + 1)
                t = s
                if 0 <= t < TILES:
                    done(pe, "vqlo", t)
                    done(pe, "exp", t - 2)
                    if t == 0:
                        pe.wait_ge(s_constr, 2)
                        pe.wait_ge(s_mod1, 2)
                    if t == 1:
                        pe.wait_ge(s_ga, 1)
                    if NT + 2 <= t < NT + 4:
                        done(pe, "x1", t - 2)
                    row0, i = t // NT * NT, t % NT
                    for first in range(0, i + 1, BT):
                        end = min(first + BT, i + 1)
                        dst = ps[:, 2 * (t % 2) + first // BT, :]
                        own = end == i + 1
                        if first > 0:
                            done(pe, "x1", t - 2)
                        for off, slot, n in key_runs(row0 + first, row0 + end):
                            masked = own and first + off + n == end
                            keys = slice(slot * P, (slot + n) * P)
                            for c in range(DC):
                                last = split3(dst[:, off * P:(off + n) * P],
                                              (qT_hi[:, t % 2, c, :], qT_lo[:, t % 2, c, :]),
                                              (xnT_hi[:, c, keys], xnT_lo[:, c, keys]), c == 0,
                                              c == DC - 1 and not masked)
                        if own:
                            last = nc.tensor.matmul(dst[:, (i - first) * P:(i - first + 1) * P], ident_r[:],
                                                    mask_r[:], start=False, stop=True)
                    last.then_inc(tl["scores"], 1)
                t = s + 2
                if 0 <= t < TILES:
                    done(pe, "xn", t)
                    done(pe, "xf", t - 1)
                    done(pe, "h2f", t - 5)
                    if t == 0:
                        pe.wait_ge(s_wqk_lo, 1)
                    if s == ROUTE + 2:
                        pe.wait_ge(s_lg, 1)
                    for c in range(DC):
                        last = nc.tensor.transpose(ps[:, Y0, c * P:(c + 1) * P], xn[:, t % 2, c * P:(c + 1) * P],
                                                   ident[:])
                    last.then_inc(tl["xT"], 1)
                t = s + 1
                if 0 <= t < TILES:
                    done(pe, "xlo", t)
                    done(pe, "vqlo", t - 1)
                    if t % NT == 0:
                        pe.wait_ge(s_wvo_lo, t // NT + 1)
                    tok = slice(slot_of(t) * P, (slot_of(t) + 1) * P)
                    for c in range(DC):
                        split3(ps[:, Y1, 0:D], (xnT_hi[:, c, tok], xnT_lo[:, c, tok]),
                               (wvo_hi[:, t // NT, c, :], wvo_lo[:, t // NT, c, :]), c == 0, c == DC - 1)
                    for m in range(DC):
                        for c in range(DC):
                            last = split3(ps[:, Y1, D + m * P:D + (m + 1) * P],
                                          (wqk_hi[:, c, m * P:(m + 1) * P], wqk_lo[:, c, m * P:(m + 1) * P]),
                                          (xnT_hi[:, c, tok], xnT_lo[:, c, tok]), c == 0, c == DC - 1)
                    last.then_inc(tl["vq"], 1)
                if s == LAST - 1:
                    cw_rows(0)
                if 0 <= s - 2 < TILES and s < LAST - 1:
                    transpose_back(s - 2)
                if s == LAST:
                    gate_up(0, 1, 1)
                    transpose_back(s - 2)
                t = s - 1
                if 0 <= t < TILES:
                    done(pe, "x1", t - 2)
                    if ROUTE - 1 <= t <= ROUTE:
                        pe.wait_ge(s_lgT, t - ROUTE + 2)
                    if t == 0:
                        pe.wait_ge(s_mod1, 4)
                    if t == 1:
                        pe.wait_ge(s_ga_raw, 1)
                    row0, i = t // NT * NT, t % NT
                    for u, first, n in units_of(t):
                        done(pe, "ptlo", u)
                        for j in range(n):
                            slot = slot_of(row0 + first + j)
                            last = split3(pv_out(t),
                                          [m[:, u % PT_RING, j * P:(j + 1) * P] for m in (pT_hi, pT_lo)],
                                          [m[:, slot, :] for m in (v_hi, v_lo)],
                                          first + j == 0, first + j == i)
                    last.then_inc(tl["pv"], 1)
                if s == LAST - 1:
                    pe.wait_ge(s_cwT, 1)
                    transpose_back(s - 2)
                    done(pe, "exp", TILES - 2)
                    gate_up(0, 0, 0)
                if s == ROUTE + 1:
                    done(pe, "h2f", s - 2)
                    logits_back(0)

            def down(k, n, first=False, final=False, drained=None):
                pe.wait_ge(s_glo, n + 1)
                if drained is not None:
                    pe.wait_ge(s_ya, drained)
                    pe.wait_ge(s_yd, drained)
                for c in range(DC):
                    cols_ = slice(W2 + c * P, W2 + (c + 1) * P)
                    last = split3(ps[:, 4 + c, :], (w_hi[k][:, cols_], w_lo[k][:, cols_]),
                                  (g_hi[:, k % 2, :], g_lo[:, k % 2, :]), first, final)
                last.then_inc(s_y, 1)

            def turn_back(b):
                pe.wait_ge(s_ya, b + 1)
                pe.wait_ge(s_yd, b + 1)
                if not (isinstance(b, int) and b == 0):
                    pe.wait_ge(s_gated, b)
                for j in range(BT):
                    for c in range(DC):
                        last = nc.tensor.transpose(
                            ps[:, TR + j // 2, (j % 2) * D + c * P:(j % 2) * D + (c + 1) * P],
                            yT[:, c, j * P:(j + 1) * P], ident[:])
                    if (isinstance(b, int) and b == NB - 1 and j == 1) or j == BT - 1:
                        last.then_inc(s_yT_mm, 1)

            def head(b, before):
                for k in range(UN):
                    n = b * EX + k
                    gate_up(b, k, n)
                    if k >= 2:
                        down(k - 2, n - 2, first=(k == 2), drained=before + 1)
                    else:
                        down(k + 2, n - 2, final=(k == 1))
                turn_back(before)

            def rest(b, first=1):
                with pe.Fori(first, NG) as g:
                    for k in range(UN):
                        n = b * EX + (g * UN + k)
                        gate_up(b, k, n)
                        down((k + 2) % UN, n - 2)

            def logits_row1():
                pe.wait_ge(s_cwT, 1)
                done(pe, "h2f", TILES - 1)
                for half in range(2):
                    logits_half(1, half, TR + half)

            for n in range(2, PEELED * UN):
                gate_up(0, n % UN, n)
                down((n - 2) % UN, n - 2, first=(n == 2))
                if n == 2:
                    transpose_back(TILES - 1)
                if n == 3:
                    logits_row1()
                if n == 4:
                    logits_back(1)
                if n == 8:
                    cw_rows(1)
            rest(0, first=PEELED)
            pe.wait_ge(s_cwT, 2)
            head(1, before=0)
            with pe.Fori(1, NB - 1) as b:
                rest(b)
                head(b + 1, before=b)
            rest(NB - 1)
            down(2, NB * EX - 2)
            down(3, NB * EX - 1, final=True)
            turn_back(NB - 1)


_INS = ['L0_attn_x', 'L0_attn_qkv', 'L0_attn_o_proj', 'L0_attn_gamma', 'L0_attn_beta', 'L0_ffn_w_router',
        'L0_ffn_we1', 'L0_ffn_we3', 'L0_ffn_we2', 'L0_ffn_ws1', 'L0_ffn_ws3', 'L0_ffn_ws2', 'L0_c', 'L0_wmod']
_OUTS = [((B, S, D), 'float32')]


def kernel(**inputs):
    import numpy as _np
    import concourse.bacc as _bacc
    from concourse import mybir as _mybir
    from concourse.bass_utils import run_bass_kernel_spmd as _run

    nc = _bacc.Bacc("TRN2", target_bir_lowering=False, num_devices=1)
    arrays, args = {}, []
    for name in _INS:
        a = _np.ascontiguousarray(inputs[name])
        arrays[f"in_{name}_dram"] = a
        args.append(nc.dram_tensor(f"in_{name}_dram", a.shape, _mybir.dt.from_np(a.dtype), kind="ExternalInput").ap())
    for i, (shape, dtype) in enumerate(_OUTS):
        dt = _mybir.dt.from_np(_np.dtype(dtype))
        args.append(nc.dram_tensor(f"out_{i}_dram", shape, dt, kind="ExternalOutput").ap())
    adaln_block(nc, *args)
    r = _run(nc, [arrays], core_ids=[0])
    return r.results[0]["out_0_dram"]
```
